# Optimizing a Trainium2 kernel written in Bass

```python
import numpy as np
import jax
import jax.numpy as jnp

def _softmax(x, axis=-1):
    return jax.nn.softmax(x, axis=axis)

def _gelu(x):
    return jax.nn.gelu(x, approximate=True)

def _silu(x):
    return jax.nn.silu(x)

def _sigmoid(x):
    return jax.nn.sigmoid(x)

def _layernorm(x, axis=-1, eps=1e-05):
    m = jnp.mean(x, axis=axis, keepdims=True)
    v = jnp.var(x, axis=axis, keepdims=True)
    return (x - m) / jnp.sqrt(v + eps)

def _scatter_add(tgt, idx, src, axis=0):
    return tgt.at[idx].add(src)

def _segment_sum(src, seg, n):
    return jax.ops.segment_sum(src, seg, n)
kernel_name = 'mk_prb_d1_jaxref_r4_8de6b6'

def setup_inputs(seed: int=0):
    np.random.seed(seed)
    _w = jnp.asarray

    def _L0_attn_setup():
        import jax, jax.numpy as jnp
        import numpy as np
        D_MODEL = 256
        N_HEADS = 32
        HEAD_DIM = D_MODEL // N_HEADS
        EPS = 1e-05
        key = jax.random.key(seed)
        ks = jax.random.split(key, 6)
        B, S = (2, 512)
        scale = 1.0 / np.sqrt(D_MODEL)
        return {'x': jax.random.normal(ks[0], (B, S, D_MODEL), dtype=jnp.float32), 'Wqkv_w': jax.random.normal(ks[1], (3 * D_MODEL, D_MODEL), dtype=jnp.float32) * scale, 'Wqkv_b': jax.random.normal(ks[2], (3 * D_MODEL,), dtype=jnp.float32) * 0.01, 'gn_w': jnp.ones((D_MODEL,), dtype=jnp.float32), 'gn_b': jnp.zeros((D_MODEL,), dtype=jnp.float32), 'out_w': jax.random.normal(ks[3], (D_MODEL, D_MODEL), dtype=jnp.float32) * scale, 'out_b': jax.random.normal(ks[4], (D_MODEL,), dtype=jnp.float32) * 0.01}
    _L0_attn_in = _L0_attn_setup()

    def _L0_ffn_setup():
        import jax, jax.numpy as jnp
        import numpy as np
        B, S, D = (4, 512, 256)
        P = 9
        DM = D // 4
        EPS = 1e-05

        def _mix(x, mix_kernel):
            xp = jnp.pad(x, ((0, 0), (1, 1), (0, 0)))
            return mix_kernel[0] * xp[:, :-2] + mix_kernel[1] * xp[:, 1:-1] + mix_kernel[2] * xp[:, 2:]

        def _layernorm(h, gamma, beta):
            mu = jnp.mean(h, axis=-1, keepdims=True)
            var = jnp.var(h, axis=-1, keepdims=True)
            return (h - mu) * jax.lax.rsqrt(var + EPS) * gamma + beta
        key = jax.random.key(seed)
        ks = jax.random.split(key, 12)
        sc_in = 1.0 / np.sqrt(D)
        sc_mid = 1.0 / np.sqrt(DM)
        return {'x': jax.random.normal(ks[0], (B, S, D), dtype=jnp.float32), 'mix_kernel': jax.random.normal(ks[1], (3, D), dtype=jnp.float32) * 0.5, 'W1': jax.random.normal(ks[2], (P, D, DM), dtype=jnp.float32) * sc_in, 'b1': jnp.zeros((P, DM), dtype=jnp.float32), 'W2': jax.random.normal(ks[3], (P, DM, D), dtype=jnp.float32) * sc_mid, 'b2': jnp.zeros((P, D), dtype=jnp.float32), 'Wo1': jax.random.normal(ks[4], (D, DM), dtype=jnp.float32) * sc_in, 'bo1': jnp.zeros((DM,), dtype=jnp.float32), 'Wo2': jax.random.normal(ks[5], (DM, P), dtype=jnp.float32) * sc_mid, 'bo2': jnp.zeros((P,), dtype=jnp.float32), 'gamma': jnp.ones((D,), dtype=jnp.float32), 'beta': jnp.zeros((D,), dtype=jnp.float32)}
    _L0_ffn_in = _L0_ffn_setup()
    _d = {'L0_attn_x': _L0_attn_in['x'], 'L0_attn_Wqkv_w': _L0_attn_in['Wqkv_w'], 'L0_attn_Wqkv_b': _L0_attn_in['Wqkv_b'], 'L0_attn_gn_w': _L0_attn_in['gn_w'], 'L0_attn_gn_b': _L0_attn_in['gn_b'], 'L0_attn_out_w': _L0_attn_in['out_w'], 'L0_attn_out_b': _L0_attn_in['out_b'], 'L0_ffn_mix_kernel': _L0_ffn_in['mix_kernel'], 'L0_ffn_W1': _L0_ffn_in['W1'], 'L0_ffn_b1': _L0_ffn_in['b1'], 'L0_ffn_W2': _L0_ffn_in['W2'], 'L0_ffn_b2': _L0_ffn_in['b2'], 'L0_ffn_Wo1': _L0_ffn_in['Wo1'], 'L0_ffn_bo1': _L0_ffn_in['bo1'], 'L0_ffn_Wo2': _L0_ffn_in['Wo2'], 'L0_ffn_bo2': _L0_ffn_in['bo2'], 'L0_ffn_gamma': _L0_ffn_in['gamma'], 'L0_ffn_beta': _L0_ffn_in['beta']}
    _x0 = _d['L0_attn_x']
    _d['L0_attn_x'] = jax.random.normal(jax.random.fold_in(jax.random.key(seed), 1), (8, 1024, 256), dtype=_x0.dtype)
    del _x0
    return _d

def reference(L0_attn_x, L0_attn_Wqkv_w, L0_attn_Wqkv_b, L0_attn_gn_w, L0_attn_gn_b, L0_attn_out_w, L0_attn_out_b, L0_ffn_mix_kernel, L0_ffn_W1, L0_ffn_b1, L0_ffn_W2, L0_ffn_b2, L0_ffn_Wo1, L0_ffn_bo1, L0_ffn_Wo2, L0_ffn_bo2, L0_ffn_gamma, L0_ffn_beta):

    def _L0_attn_ref(x, Wqkv_w, Wqkv_b, gn_w, gn_b, out_w, out_b):
        import jax, jax.numpy as jnp
        import numpy as np
        D_MODEL = 256
        N_HEADS = 32
        HEAD_DIM = D_MODEL // N_HEADS
        EPS = 1e-05
        B, S, Dm = x.shape
        H, Dh = (N_HEADS, HEAD_DIM)
        qkv = x @ Wqkv_w.T + Wqkv_b
        qkv = qkv.reshape(B, S, 3, H, Dh)
        q, k, v = (qkv[:, :, 0], qkv[:, :, 1], qkv[:, :, 2])
        a = jnp.einsum('bthd,bshd->bhts', q, k)
        ctx = jnp.einsum('bhts,bshd->bthd', a, v)
        g = ctx.transpose(0, 2, 3, 1)
        mean = g.mean(axis=(2, 3), keepdims=True)
        var = ((g - mean) ** 2).mean(axis=(2, 3), keepdims=True)
        gh = (g - mean) * jax.lax.rsqrt(var + EPS)
        gh = gh * gn_w.reshape(H, Dh, 1) + gn_b.reshape(H, Dh, 1)
        ctx = gh.transpose(0, 3, 1, 2).reshape(B, S, Dm)
        return ctx @ out_w.T + out_b

    def _L0_ffn_ref(x, mix_kernel, W1, b1, W2, b2, Wo1, bo1, Wo2, bo2, gamma, beta):
        import jax, jax.numpy as jnp
        import numpy as np
        B, S, D = (4, 512, 256)
        P = 9
        DM = D // 4
        EPS = 1e-05

        def _mix(x, mix_kernel):
            xp = jnp.pad(x, ((0, 0), (1, 1), (0, 0)))
            return mix_kernel[0] * xp[:, :-2] + mix_kernel[1] * xp[:, 1:-1] + mix_kernel[2] * xp[:, 2:]

        def _layernorm(h, gamma, beta):
            mu = jnp.mean(h, axis=-1, keepdims=True)
            var = jnp.var(h, axis=-1, keepdims=True)
            return (h - mu) * jax.lax.rsqrt(var + EPS) * gamma + beta
        x_mixed = _mix(x, mix_kernel)
        h = jnp.einsum('bsd,pdm->bspm', x_mixed, W1) + b1
        stacked_paths = jnp.einsum('bspm,pmd->bspd', h, W2) + b2
        scores = jnp.tanh(x_mixed @ Wo1 + bo1) @ Wo2 + bo2
        idx = jnp.argmax(scores, axis=-1)
        weights = jax.nn.one_hot(idx, P, dtype=stacked_paths.dtype)
        collapsed = jnp.einsum('bspd,bsp->bsd', stacked_paths, weights)
        return _layernorm(x + collapsed, gamma, beta)
    x = L0_attn_x
    xn = _layernorm(x, axis=-1)
    x = x + _L0_attn_ref(xn, L0_attn_Wqkv_w, L0_attn_Wqkv_b, L0_attn_gn_w, L0_attn_gn_b, L0_attn_out_w, L0_attn_out_b) + _L0_ffn_ref(xn, L0_ffn_mix_kernel, L0_ffn_W1, L0_ffn_b1, L0_ffn_W2, L0_ffn_b2, L0_ffn_Wo1, L0_ffn_bo1, L0_ffn_Wo2, L0_ffn_bo2, L0_ffn_gamma, L0_ffn_beta)
    return x

_drawn_inputs = setup_inputs


def setup_inputs(seed=0):
    import zlib

    import numpy as np

    out = dict(_drawn_inputs(seed))
    spreads = {'L0_attn_gn_w': (1.0, 0.2),
     'L0_attn_gn_b': (0.0, 0.1),
     'L0_ffn_b1': (0.0, 0.1),
     'L0_ffn_b2': (0.0, 0.1),
     'L0_ffn_bo1': (0.0, 0.1),
     'L0_ffn_bo2': (0.0, 0.1),
     'L0_ffn_gamma': (1.0, 0.2),
     'L0_ffn_beta': (0.0, 0.1)}
    factors = {'L0_attn_Wqkv_b': 8.0, 'L0_attn_out_b': 8.0}
    for name, (base, spread) in spreads.items():
        noise = np.random.default_rng([zlib.crc32(name.encode()), seed]).standard_normal(out[name].shape)
        drawn = base * np.exp(spread * noise) if base else spread * noise
        out[name] = jnp.asarray(drawn.astype(out[name].dtype))
    for name, factor in factors.items():
        out[name] = (out[name] * factor).astype(out[name].dtype)
    return out
```

```python
from contextlib import ExitStack

import concourse.bass as bass
from concourse import mybir

ALU = mybir.AluOpType
ACT = mybir.ActivationFunctionType
F32 = mybir.dt.float32
F32R = mybir.dt.float32r
BF16 = mybir.dt.bfloat16
AX_X = mybir.AxisListType.X
EPS = 1e-5

P = 128
GROUP = 4
GROUPS = 2
PAIRS = 4
GT = GROUP * P
SLOTS = 3


def block_kernel(nc, x, wqkv_t, wq, out_wt, w1, w2, wo2, b2, cols, rows, gamma, beta, out_b, bo2, consts, experts, out):
    B, S, D = x.shape
    E = b2.shape[0]
    DM = wo2.shape[0]
    DC = D // P
    NJ = (E + 1) * DM // P
    LAST = NJ - 1
    RK = DM + E
    DC2 = 2 * D
    assert (P, GT * GROUPS, DC, NJ, 2 * DM) == (128, S, 2, 5, P) and B % 2 == 0

    x_dram = x.rearrange("b (p t i) d -> b p i t d", i=P, t=2)
    out_dram = out.rearrange("b (p t i) d -> b p i t d", i=P, t=2)

    ctx = ExitStack()
    with ctx:
        def sb(name, shape, dt=F32):
            return ctx.enter_context(nc.sbuf_tensor(name, shape, dt))

        def sem(name):
            return ctx.enter_context(nc.semaphore(name))

        wqkvT_sb = sb("wqkvT_sb", [P, DC, 3 * D])
        wq_sb = sb("wq_sb", [P, DC, D])
        outwT_sb = sb("outwT_sb", [P, DC, D])
        w1_hi = sb("w1_hi", [P, DC, NJ * P], F32R)
        w1_lo = sb("w1_lo", [P, DC, NJ * P], F32R)
        w2_hi = sb("w2_hi", [P, NJ, D], F32R)
        w2_lo = sb("w2_lo", [P, NJ, D], F32R)
        wo2_sb = sb("wo2_sb", [P, E])
        b2_sb = sb("b2_sb", [P, D])
        path_bias = sb("path_bias", [P, D])
        b1_blocks = sb("b1_blocks", [P, NJ, E])
        cols_sb = sb("cols_sb", [P, cols.shape[1]])
        rows_sb = sb("rows_sb", [1, rows.shape[1]])
        gamma_sb = sb("gamma_sb", [P, D])
        bo2_sb = sb("bo2_sb", [P, E])
        consts_sb = sb("consts_sb", [P, consts.shape[1]])
        experts_sb = sb("experts_sb", [P, NJ * P])
        spread = sb("spread", [P, NJ * P], F32R)
        ident_bf = sb("ident_bf", [P, P], BF16)
        bk_tokens = sb("bk_tokens", [1, D])
        outb_sb = sb("outb_sb", [P, D])
        row_bias = sb("row_bias", [P, D])
        ident = consts_sb[:, 0:P]
        head_mask = consts_sb[:, P:2 * P]
        head_mean = consts_sb[:, 2 * P:3 * P]
        ones_col = consts_sb[:, 3 * P:3 * P + 1]
        minus_half = consts_sb[:, 3 * P + 1:3 * P + 2]
        rank = consts_sb[:, 3 * P + 2:3 * P + 2 + E]
        path_of = consts_sb[:, 3 * P + 2 + E:3 * P + 2 + E + NJ * E].rearrange("p (j e) -> p j e", e=E)
        bq_col, gnw_col, gnb_col = cols_sb[:, 0:2], cols_sb[:, 2:4], cols_sb[:, 4:6]
        tap_col = cols_sb[:, 6:12].rearrange("p (j c) -> p j c", c=DC)
        b1_col, bo1_col = cols_sb[:, 12:12 + NJ], cols_sb[:, 12 + NJ:13 + NJ]
        bk_row, bv_row = rows_sb[:, 0:D], rows_sb[:, D:2 * D]

        x_sb = [sb(f"x_sb{q}", [P, 2 * PAIRS, D]) for q in range(2)]
        xn = [sb(f"xn{q}", [P, 2 * PAIRS, D]) for q in range(2)]
        xn_hi = sb("xn_hi", [P, GROUP, D], F32R)
        xn_lo = sb("xn_lo", [P, GROUP, D], F32R)
        xnT = [sb(f"xnT{q}", [P, DC, S + 2]) for q in range(2)]
        col_sum = [sb(f"col_sum{q}", [P, DC, GROUPS]) for q in range(2)]
        x_stats = sb("x_stats", [P, GROUPS, GROUP, 6])
        x_mv = sb("x_mv", [P, GROUPS, GROUP, 2])
        x_var = sb("x_var", [P, GROUPS, GROUP])
        x_rstd = sb("x_rstd", [P, GROUPS, GROUP])
        x_shift = sb("x_shift", [P, GROUPS, GROUP])
        xm = sb("xm", [P, GROUPS, DC, GT])
        xm_hi = sb("xm_hi", [P, GROUPS, DC, GT], F32R)
        xm_lo = sb("xm_lo", [P, GROUPS, DC, GT], F32R)
        h_sb = sb("h_sb", [P, SLOTS, GT])
        hm = sb("hm", [P, SLOTS, GT])
        hm_hi = [sb(f"hm_hi{g}", [P, NJ, GT], F32R) for g in range(GROUPS)]
        hm_lo = [sb(f"hm_lo{g}", [P, NJ, GT], F32R) for g in range(GROUPS)]
        score = sb("score", [P, GROUP, E])
        best = sb("best", [P, GROUP])
        tied = sb("tied", [P, GROUP, E])
        onehot = sb("onehot", [P, GROUP, E], BF16)
        z = sb("z", [P, 2, 2, D])
        z_stats = sb("z_stats", [P, PAIRS, 2, 6])
        z_mv = sb("z_mv", [P, PAIRS, 2, 2])
        z_var = sb("z_var", [P, PAIRS, 2])
        z_rstd = sb("z_rstd", [P, PAIRS, 2])
        out_sb = sb("out_sb", [P, 2, 2, D])
        tok_sum = sb("tok_sum", [P, DC])
        sum_row = sb("sum_row", [1, 2, D])
        q_cols = sb("q_cols", [P, DC, 2])
        k_row = sb("k_row", [1, D])
        v_row = sb("v_row", [1, D])
        gram = sb("gram", [P, DC, D])
        gram_v = sb("gram_v", [P, DC, D])
        kv = sb("kv", [P, DC, P])
        mapT = sb("mapT", [P, DC, D])
        map_ = sb("map_", [P, DC, D])
        quad = gram_v
        stat = sb("stat", [P, 6])
        head_avg = sb("head_avg", [P, DC])
        dev = sb("dev", [P, DC])
        second = sb("second", [P, DC])
        head_var = sb("head_var", [P, DC])
        head_rstd = sb("head_rstd", [P, DC])
        gn_scale = sb("gn_scale", [P, DC])
        gn_shift = sb("gn_shift", [P, DC])
        outw_scaled = map_
        attn_mat = sb("attn_mat", [P, DC, D])
        attn_row = sb("attn_row", [P, D])

        ps_t, ps_gram, ps_chain, ps_h0, ps_h1, ps_mask, ps_ffn, ps_attn = [
            ctx.enter_context(nc.psum_tensor(n, [P, 512], F32))
            for n in ("ps_t", "ps_gram", "ps_chain", "ps_h0", "ps_h1", "ps_mask", "ps_ffn", "ps_attn")]
        ps_h = [ps_h0, ps_h1]

        consts_in = sem("consts_in")
        weights_in = sem("weights_in")
        w1_in, w2_in = sem("w1_in"), sem("w2_in")
        x_in = [[sem(f"x_in{q}{g}") for g in range(GROUPS)] for q in range(2)]
        prep = sem("prep")
        bias_prod = sem("bias_prod")
        w1_hi_made, w2_hi_made = sem("w1_hi_made"), sem("w2_hi_made")
        stats_chain = sem("stats_chain")
        var_ready = sem("var_ready")
        rstd_ready = sem("rstd_ready")
        shift_ready = sem("shift_ready")
        xn_ready = sem("xn_ready")
        t_ready = sem("t_ready")
        xnT_ready = sem("xnT_ready")
        xn_hi_ready = sem("xn_hi_ready")
        xn_lo_ready = sem("xn_lo_ready")
        gram_used = sem("gram_used")
        gram_done = sem("gram_done")
        gram_read = sem("gram_read")
        center_ready = sem("center_ready")
        left_done = sem("left_done")
        xm_ready = sem("xm_ready")
        xm_hi_ready = sem("xm_hi_ready")
        xm_lo_ready = sem("xm_lo_ready")
        h_ready = sem("h_ready")
        router_hidden = sem("router_hidden")
        h_copied = sem("h_copied")
        scores_ready = sem("scores_ready")
        router_chain = sem("router_chain")
        onehot_ready = sem("onehot_ready")
        route_ready = sem("route_ready")
        route_copied = sem("route_copied")
        mask_ready = sem("mask_ready")
        masked = sem("masked")
        hm_hi_ready = sem("hm_hi_ready")
        hm_lo_ready = sem("hm_lo_ready")
        ffn_ready = sem("ffn_ready")
        z_done = sem("z_done")
        z_chain = sem("z_chain")
        z_var_ready = sem("z_var_ready")
        z_rstd_ready = sem("z_rstd_ready")
        attn_ready = sem("attn_ready")
        u_done = sem("u_done")
        out_ready = sem("out_ready")
        stored = [sem(f"stored{s}") for s in range(2)]
        tok_sum_ready = sem("tok_sum_ready")
        chain_pe = sem("chain_pe")
        chain_read = sem("chain_read")
        small_chain = sem("small_chain")
        head_var_ready = sem("head_var_ready")
        head_rstd_ready = sem("head_rstd_ready")
        scaled_ready = sem("scaled_ready")
        x_biased = sem("x_biased")

        ORDER = [LAST] + list(range(LAST))
        NSTAGE = 13
        WEIGHT_DMAS = 12
        CREDIT = 1

        def batches(eng, first, step, tail):
            first(0, 0, 0)
            step(0, 0, (1, 0), None)
            with eng.Fori(0, B // 2 - 1) as i:
                step(i * 2 + 1, 1, (i * 2 + 2, i + 1), i * 2)
                step(i * 2 + 2, 0, (i * 2 + 3, i + 1), i * 2 + 1)
            step(B - 1, 1, None, B - 2)
            tail(B - 1, 1)

        block = ctx.enter_context(nc.Block())

        @block.sync
        def _(sp):
            def load(nb, q, g):
                for p in (2 * g, 2 * g + 1):
                    sp.dma_start(x_sb[q][:, 2 * p:2 * p + 2, :], x_dram[nb, p]).then_inc(x_in[q][g], 16)

            load(0, 0, 0)
            sp.dma_start(consts_sb[:, :], consts).then_inc(consts_in, 16)
            sp.dma_start(cols_sb[:, :], cols).then_inc(weights_in, 16)
            load(0, 0, 1)
            sp.dma_start(h_flat(h_sb)[:, 0:DC * NJ * P].rearrange("p (c n) -> p c n", c=DC),
                         w1.rearrange("(c p) n -> p c n", p=P)).then_inc(w1_in, 16)
            sp.dma_start(h_flat(hm)[:, 0:LAST * D].rearrange("p (j n) -> p j n", n=D),
                         w2[0:LAST * P, :].rearrange("(j p) n -> p j n", p=P)).then_inc(w2_in, 16)
            sp.dma_start(h_flat(hm)[0:DM, LAST * D:NJ * D], w2[LAST * P:E * DM, :]).then_inc(w2_in, 16)
            sp.dma_start(rows_sb[:, :], rows).then_inc(weights_in, 16)
            sp.dma_start(experts_sb[DM:RK, :], experts).then_inc(weights_in, 16)
            sp.dma_start(wo2_sb[DM:P, :], wo2).then_inc(weights_in, 16)
            sp.dma_start(b2_sb[DM:RK, :], b2).then_inc(weights_in, 16)
            sp.dma_start(bo2_sb[:, :], bo2).then_inc(weights_in, 16)
            sp.dma_start(gamma_sb[:, :], gamma).then_inc(weights_in, 16)
            sp.dma_start(row_bias[:, :], beta).then_inc(weights_in, 16)
            sp.dma_start(outb_sb[:, :], out_b).then_inc(weights_in, 16)
            sp.dma_start(wqkvT_sb[:, :, :], wqkv_t.rearrange("(c p) n -> p c n", p=P)).then_inc(weights_in, 16)
            sp.dma_start(wq_sb[:, :, :], wq.rearrange("(c p) n -> p c n", p=P)).then_inc(weights_in, 16)
            sp.dma_start(outwT_sb[:, :, :], out_wt.rearrange("(c p) n -> p c n", p=P)).then_inc(weights_in, 16)

            def store(b, p):
                sp.wait_ge(out_ready, CREDIT + PAIRS * b + p + 1)
                sp.dma_start(out_dram[b, p], out_sb[:, p % 2, :, :]).then_inc(stored[p % 2], 16)

            def first(nb, half, q):
                pass

            def step(b, q, nxt, prev):
                if nxt:
                    if prev is not None:
                        sp.wait_ge(out_ready, CREDIT + PAIRS * prev + 2)
                    load(nxt[0], 1 - q, 0)
                if prev is not None:
                    store(prev, 2)
                    store(prev, 3)
                if nxt:
                    load(nxt[0], 1 - q, 1)
                store(b, 0)
                store(b, 1)

            def tail(b, q):
                store(b, 2)
                store(b, 3)

            batches(sp, first, step, tail)
            for s in range(2):
                sp.wait_ge(stored[s], 16 * (CREDIT + 2 * B))

        @block.gpsimd
        def _(pool):
            pool.wait_ge(consts_in, 16)

            def x_pow(nb, g):
                pool.wait_ge(var_ready, 2 * nb + g + 1)
                nc.gpsimd.tensor_tensor(x_rstd[:, g, :], x_var[:, g, :],
                                        minus_half.to_broadcast([P, GROUP]), ALU.pow).then_inc(rstd_ready, 1)

            def normalise(nb, q, g):
                pool.wait_ge(shift_ready, 2 * nb + g + 1)
                pool.nop(nofuse=True)
                for t in range(GROUP):
                    nc.gpsimd.tensor_scalar(xn[q][:, GROUP * g + t, :], x_sb[q][:, GROUP * g + t, :],
                                            x_rstd[:, g, t:t + 1], x_shift[:, g, t:t + 1],
                                            ALU.mult, ALU.add).then_inc(xn_ready, 1)

            def mixed_low(b, g):
                for c in range(DC):
                    pool.wait_ge(xm_hi_ready, 4 * b + 2 * g + c + 1)
                    nc.gpsimd.tensor_tensor(xm_lo[:, g, c, :], xm[:, g, c, :], xm_hi[:, g, c, :].bitcast(F32),
                                            ALU.subtract).then_inc(xm_lo_ready, 1)

            def hidden_low(b, g, k):
                j = ORDER[k]
                r = DM if j == LAST else P
                pool.wait_ge(hm_hi_ready, 10 * b + NJ * g + k + 1)
                nc.gpsimd.tensor_tensor(hm_lo[g][0:r, j, :], hm[0:r, k % SLOTS, :], hm_hi[g][0:r, j, :].bitcast(F32),
                                        ALU.subtract).then_inc(hm_lo_ready, 1)

            def z_pow(b, p):
                pool.wait_ge(z_var_ready, 4 * b + p + 1)
                nc.gpsimd.tensor_tensor(z_rstd[:, p, :], z_var[:, p, :], minus_half.to_broadcast([P, 2]),
                                        ALU.pow).then_inc(z_rstd_ready, 1)

            def bias_x(b, q, p):
                pool.wait_ge(chain_read, CREDIT + NSTAGE * (b + 1))
                nc.gpsimd.tensor_tensor(x_sb[q][:, 2 * p:2 * p + 2, :], x_sb[q][:, 2 * p:2 * p + 2, :],
                                        attn_row[:, :].rearrange("p (o n) -> p o n", o=1).to_broadcast([P, 2, D]),
                                        ALU.add).then_inc(x_biased, 1)

            def final(b, q, p):
                pool.wait_ge(x_biased, 4 * b + p + 1)
                pool.wait_ge(u_done, CREDIT + 4 * b + p + 1)
                nc.gpsimd.tensor_tensor(out_sb[:, p % 2, :, :], out_sb[:, p % 2, :, :],
                                        x_sb[q][:, 2 * p:2 * p + 2, :], ALU.add).then_inc(out_ready, 1)

            def head_pow(b):
                pool.wait_ge(head_var_ready, b + 1)
                nc.gpsimd.tensor_tensor(head_rstd[:, :], head_var[:, :], minus_half.to_broadcast([P, DC]),
                                        ALU.pow).then_inc(head_rstd_ready, 1)

            def first(nb, half, q):
                for g in range(GROUPS):
                    x_pow(nb, g)
                    normalise(nb, q, g)
                mixed_low(nb, 0)

            def step(b, q, nxt, prev):
                if prev is not None:
                    z_pow(prev, 2)
                    bias_x(prev, 1 - q, 2)
                hidden_low(b, 0, 0)
                if nxt:
                    x_pow(nxt[0], 0)
                if prev is not None:
                    final(prev, 1 - q, 2)
                if nxt:
                    normalise(nxt[0], 1 - q, 0)
                mixed_low(b, 1)
                hidden_low(b, 0, 1)
                hidden_low(b, 0, 2)
                if prev is not None:
                    bias_x(prev, 1 - q, 3)
                hidden_low(b, 0, 3)
                if prev is not None:
                    z_pow(prev, 3)
                hidden_low(b, 0, 4)
                if prev is not None:
                    final(prev, 1 - q, 3)
                head_pow(b)
                if nxt:
                    x_pow(nxt[0], 1)
                    normalise(nxt[0], 1 - q, 1)
                z_pow(b, 0)
                hidden_low(b, 1, 0)
                hidden_low(b, 1, 1)
                bias_x(b, q, 0)
                final(b, q, 0)
                hidden_low(b, 1, 2)
                hidden_low(b, 1, 3)
                if nxt:
                    mixed_low(nxt[0], 0)
                z_pow(b, 1)
                hidden_low(b, 1, 4)
                bias_x(b, q, 1)
                final(b, q, 1)

            def tail(b, q):
                for p in (2, 3):
                    z_pow(b, p)
                    bias_x(b, q, p)
                    final(b, q, p)

            batches(pool, first, step, tail)

        @block.scalar
        def _(act):
            def weights_high():
                act.wait_ge(w1_in, 16)
                nc.scalar.activation(w1_hi[:, :, :],
                                     h_flat(h_sb)[:, 0:DC * NJ * P].rearrange("p (c n) -> p c n", c=DC),
                                     ACT.Copy).then_inc(w1_hi_made, 1)
                act.wait_ge(w2_in, 32)
                nc.scalar.activation(w2_hi[:, 0:LAST, :],
                                     h_flat(hm)[:, 0:LAST * D].rearrange("p (j n) -> p j n", n=D), ACT.Copy)
                nc.scalar.activation(w2_hi[0:DM, LAST, :], h_flat(hm)[0:DM, LAST * D:NJ * D],
                                     ACT.Copy).then_inc(w2_hi_made, 1)

            def xn_high(nb, q, g):
                if not (isinstance(nb, int) and nb == 0 and g == 0):
                    act.wait_ge(gram_used, 2 * nb + g)
                for half in range(2):
                    act.wait_ge(xn_ready, 8 * nb + GROUP * g + 2 * half + 2)
                    nc.scalar.activation(xn_hi[:, 2 * half:2 * half + 2, :],
                                         xn[q][:, GROUP * g + 2 * half:GROUP * g + 2 * half + 2, :],
                                         ACT.Copy).then_inc(xn_hi_ready, 1)

            def transposed(nb, q, g, c):
                act.wait_ge(t_ready, 4 * nb + 2 * g + c + 1)
                nc.scalar.activation(xnT[q][:, c, 1 + GT * g:1 + GT * (g + 1)], ps_t[:, :], ACT.Copy,
                                     accum_out=col_sum[q][:, c, g:g + 1]).then_inc(xnT_ready, 1)

            def center(b, q, g):
                act.wait_ge(xnT_ready, 4 * b + 4)
                for c in range(DC):
                    nc.scalar.activation(xm[:, g, c, :], xnT[q][:, c, 1 + GT * g:1 + GT * (g + 1)], ACT.Copy,
                                         scale=tap_col[:, 1, c:c + 1]).then_inc(center_ready, 1)

            def mixed_high(b, g):
                for c in range(DC):
                    act.wait_ge(xm_ready, 4 * b + 2 * g + c + 1)
                    nc.scalar.activation(xm_hi[:, g, c, :], xm[:, g, c, :], ACT.Copy).then_inc(xm_hi_ready, 1)

            def hidden(b, g, k):
                n = 10 * b + NJ * g + k
                act.wait_ge(h_ready, n + 1)
                src = ps_h[(NJ * g + k) % 2]
                if k == 0:
                    nc.scalar.activation(h_sb[DM:P, 0, :], src[DM:P, :], ACT.Tanh,
                                         bias=bo1_col[DM:P, :]).then_inc(router_hidden, 1)
                    nc.scalar.activation(h_sb[0:DM, 0, :], src[0:DM, :], ACT.Copy).then_inc(h_copied, 1)
                else:
                    nc.scalar.activation(h_sb[:, k % SLOTS, :], src[:, :], ACT.Copy).then_inc(h_copied, 1)

            def route(b, g):
                act.wait_ge(route_ready, 2 * b + g + 1)
                nc.scalar.activation(hm_hi[g][DM:RK, LAST, :], ps_mask[DM:RK, :], ACT.Copy).then_inc(route_copied, 1)

            def hidden_high(b, g, k):
                j = ORDER[k]
                r = DM if j == LAST else P
                act.wait_ge(masked, CREDIT + 10 * b + NJ * g + k + 1)
                nc.scalar.activation(hm_hi[g][0:r, j, :], hm[0:r, k % SLOTS, :], ACT.Copy).then_inc(hm_hi_ready, 1)

            def read_stage(b, s, dst):
                act.wait_ge(chain_pe, NSTAGE * b + s + 1)
                nc.scalar.activation(dst, ps_chain[:, :].rearrange("p (c n) -> p c n", c=DC),
                                     ACT.Copy).then_inc(chain_read, 1)

            def read_gram(b):
                act.wait_ge(gram_done, b + 1)
                nc.scalar.activation(gram[:, 0, :], ps_gram[:, 0:D], ACT.Copy)
                nc.scalar.activation(gram[:, 1, P:D], ps_gram[:, D:D + P], ACT.Copy).then_inc(gram_read, 1)

            def first(nb, half, q):
                for g in range(GROUPS):
                    for c in range(DC):
                        transposed(nb, q, g, c)
                    xn_high(nb, q, g)
                    if g == 0:
                        weights_high()
                act.wait_ge(weights_in, 16 * WEIGHT_DMAS)
                center(nb, q, 0)
                mixed_high(nb, 0)
                act.wait_ge(prep, 6)

            def step(b, q, nxt, prev):
                hidden(b, 0, 0)
                center(b, q, 1)
                read_gram(b)
                route(b, 0)
                hidden(b, 0, 1)
                hidden_high(b, 0, 0)
                read_stage(b, 3, gram_v[:, :, :])
                hidden(b, 0, 2)
                hidden_high(b, 0, 1)
                mixed_high(b, 1)
                hidden_high(b, 0, 2)
                read_stage(b, 5, mapT[:, :, :])
                if nxt:
                    transposed(nxt[0], 1 - q, 0, 0)
                    xn_high(nxt[0], 1 - q, 0)
                hidden(b, 0, 3)
                hidden_high(b, 0, 3)
                read_stage(b, 6, map_[:, :, :])
                if nxt:
                    transposed(nxt[0], 1 - q, 0, 1)
                hidden(b, 0, 4)
                hidden_high(b, 0, 4)
                hidden(b, 1, 0)
                route(b, 1)
                hidden(b, 1, 1)
                hidden_high(b, 1, 0)
                read_stage(b, 11, attn_mat[:, :, :])
                hidden(b, 1, 2)
                hidden_high(b, 1, 1)
                if nxt:
                    transposed(nxt[0], 1 - q, 1, 0)
                hidden_high(b, 1, 2)
                if nxt:
                    transposed(nxt[0], 1 - q, 1, 1)
                    center(nxt[0], 1 - q, 0)
                    xn_high(nxt[0], 1 - q, 1)
                hidden(b, 1, 3)
                hidden_high(b, 1, 3)
                if nxt:
                    mixed_high(nxt[0], 0)
                hidden(b, 1, 4)
                hidden_high(b, 1, 4)

            def tail(b, q):
                pass

            batches(act, first, step, tail)

        @block.vector
        def _(dve):
            def link(ins, s, value):
                ins.then_inc(s, 1)
                dve.wait_ge(s, value)

            free = [(masked, 1), (z_done, 1), (u_done, 1), (chain_read, 1), (h_copied, 1), (out_ready, 1),
                    (stored[0], 16), (stored[1], 16)]
            edges = [xnT[q][:, c, at:at + 1] for q in range(2) for c in range(DC) for at in (0, S + 1)]
            for edge, (s, credit) in zip(edges, free):
                nc.vector.memset(edge, 0.0).then_inc(s, credit)

            def constants():
                dve.wait_ge(w1_hi_made, 1)
                link(nc.vector.tensor_tensor(w1_lo[:, :, :],
                                             h_flat(h_sb)[:, 0:DC * NJ * P].rearrange("p (c n) -> p c n", c=DC),
                                             w1_hi[:, :, :].bitcast(F32), ALU.subtract), prep, 1)
                dve.wait_ge(weights_in, 16 * WEIGHT_DMAS)
                dve.wait_ge(consts_in, 16)
                nc.vector.tensor_copy(ident_bf[:, :], ident)
                nc.vector.tensor_copy(spread[DM:RK, :], experts_sb[DM:RK, :])
                for c in range(DC):
                    nc.vector.tensor_copy(q_cols[:, c, 1:2], bq_col[:, c:c + 1])
                nc.vector.tensor_scalar(bk_tokens[:, :], bk_row, float(S), None, ALU.mult)
                nc.vector.tensor_tensor(row_bias[:, :], row_bias[:, :], outb_sb[:, :], ALU.add)
                link(nc.vector.tensor_tensor(b1_blocks[:, :, :], path_of,
                                             b1_col.rearrange("p (j a) -> p j a", a=1).to_broadcast([P, NJ, E]),
                                             ALU.mult), prep, 2)

            def path_biases():
                dve.wait_ge(w2_hi_made, 1)
                nc.vector.tensor_tensor(w2_lo[:, 0:LAST, :],
                                        h_flat(hm)[:, 0:LAST * D].rearrange("p (j n) -> p j n", n=D),
                                        w2_hi[:, 0:LAST, :].bitcast(F32), ALU.subtract)
                link(nc.vector.tensor_tensor(w2_lo[0:DM, LAST, :], h_flat(hm)[0:DM, LAST * D:NJ * D],
                                             w2_hi[0:DM, LAST, :].bitcast(F32), ALU.subtract), prep, 3)
                dve.wait_ge(bias_prod, 1)
                link(nc.vector.tensor_tensor(path_bias[DM:RK, :], ps_chain[DM:RK, 0:D], b2_sb[DM:RK, :], ALU.add),
                     prep, 4)
                link(nc.vector.tensor_copy(w2_hi[DM:RK, LAST, :], path_bias[DM:RK, :]), prep, 5)
                link(nc.vector.tensor_tensor(w2_lo[DM:RK, LAST, :], path_bias[DM:RK, :],
                                             w2_hi[DM:RK, LAST, :].bitcast(F32), ALU.subtract), prep, 6)

            def x_statistics(nb, half, q, g):
                dve.wait_ge(x_in[q][g], 32 * (half + 1))
                for t in range(GROUP):
                    last = nc.vector.bn_stats(x_stats[:, g, t, :], x_sb[q][:, GROUP * g + t, :])
                link(last, stats_chain, 4 * nb + 2 * g + 1)
                dve.nop(nofuse=True)
                for t in range(GROUP):
                    last = nc.vector.bn_aggr(x_mv[:, g, t, :], x_stats[:, g, t, :])
                link(last, stats_chain, 4 * nb + 2 * g + 2)
                nc.vector.tensor_scalar(x_var[:, g, :], x_mv[:, g, :, 1], EPS, None, ALU.add).then_inc(var_ready, 1)

            def xn_low(nb, q, g):
                for half in range(2):
                    n = 4 * nb + 2 * g + half + 1
                    dve.wait_ge(xn_hi_ready, n)
                    nc.vector.tensor_tensor(xn_lo[:, 2 * half:2 * half + 2, :],
                                            xn[q][:, GROUP * g + 2 * half:GROUP * g + 2 * half + 2, :],
                                            xn_hi[:, 2 * half:2 * half + 2, :].bitcast(F32),
                                            ALU.subtract).then_inc(xn_lo_ready, 1)

            def x_offset(nb, g):
                dve.wait_ge(rstd_ready, 2 * nb + g + 1)
                nc.vector.scalar_tensor_tensor(x_shift[:, g, :], x_mv[:, g, :, 0], -1.0, x_rstd[:, g, :],
                                               ALU.mult, ALU.mult).then_inc(shift_ready, 1)

            def mix(b, q, g):
                for c in range(DC):
                    n = 4 * b + 2 * g + c + 1
                    dve.wait_ge(center_ready, n)
                    link(nc.vector.scalar_tensor_tensor(xm[:, g, c, :], xnT[q][:, c, GT * g:GT * (g + 1)],
                                                        tap_col[:, 0, c:c + 1], xm[:, g, c, :],
                                                        ALU.mult, ALU.add), left_done, n)
                    nc.vector.scalar_tensor_tensor(xm[:, g, c, :], xnT[q][:, c, 2 + GT * g:2 + GT * (g + 1)],
                                                   tap_col[:, 2, c:c + 1], xm[:, g, c, :],
                                                   ALU.mult, ALU.add).then_inc(xm_ready, 1)

            def choose(b, g):
                n = 10 * b + 5 * g
                dve.wait_ge(scores_ready, 2 * b + g + 1)

                def over_paths(a):
                    return a.rearrange("p (t o) -> p t o", o=1).to_broadcast([P, GROUP, E])

                link(nc.vector.tensor_tensor(score[:, :, :], ps_mask[:, 0:GROUP * E].rearrange("p (t e) -> p t e", e=E),
                                             bo2_sb[:, :].rearrange("p (o e) -> p o e", o=1).to_broadcast([P, GROUP, E]),
                                             ALU.add), router_chain, n + 1)
                link(nc.vector.tensor_reduce(best[:, :], score[:, :, :], AX_X, ALU.max), router_chain, n + 2)
                link(nc.vector.tensor_tensor(tied[:, :, :], score[:, :, :], over_paths(best[:, :]), ALU.is_equal),
                     router_chain, n + 3)
                link(nc.vector.tensor_tensor(tied[:, :, :], tied[:, :, :],
                                             rank.rearrange("p (o e) -> p o e", o=1).to_broadcast([P, GROUP, E]),
                                             ALU.mult), router_chain, n + 4)
                link(nc.vector.tensor_reduce(best[:, :], tied[:, :, :], AX_X, ALU.max), router_chain, n + 5)
                nc.vector.tensor_tensor(onehot[:, :, :], tied[:, :, :], over_paths(best[:, :]),
                                        ALU.is_equal).then_inc(onehot_ready, 1)

            def mask(b, g, k):
                n = 10 * b + NJ * g + k + 1
                j = ORDER[k]
                r = DM if j == LAST else P
                dve.wait_ge(h_copied, CREDIT + n)
                dve.wait_ge(mask_ready, n)
                if not (isinstance(n, int) and n <= SLOTS):
                    dve.wait_ge(hm_lo_ready, n - SLOTS)
                nc.vector.tensor_tensor(hm[0:r, k % SLOTS, :], h_sb[0:r, k % SLOTS, :], ps_mask[0:r, :], ALU.mult).then_inc(masked, 1)

            def z_statistics(b, q, p):
                n = 4 * b + p + 1
                dve.wait_ge(ffn_ready, n)
                link(nc.vector.tensor_tensor(z[:, p % 2, :, :], ps_ffn[:, :].rearrange("p (t n) -> p t n", t=2),
                                             xn[q][:, 2 * p:2 * p + 2, :], ALU.add), z_done, CREDIT + n)
                for t in range(2):
                    last = nc.vector.bn_stats(z_stats[:, p, t, :], z[:, p % 2, t, :])
                link(last, z_chain, 3 * n - 2)
                dve.nop(nofuse=True)
                for t in range(2):
                    last = nc.vector.bn_aggr(z_mv[:, p, t, :], z_stats[:, p, t, :])
                link(last, z_chain, 3 * n - 1)
                nc.vector.tensor_scalar(z_var[:, p, :], z_mv[:, p, :, 1], EPS, None, ALU.add).then_inc(z_var_ready, 1)
                for t in range(2):
                    last = nc.vector.scalar_tensor_tensor(z[:, p % 2, t, :], z[:, p % 2, t, :], z_mv[:, p, t, 0:1],
                                                          gamma_sb[:, :], ALU.subtract, ALU.mult)
                link(last, z_chain, 3 * n)

            def combine(b, p):
                n = 4 * b + p + 1
                dve.wait_ge(z_rstd_ready, n)
                dve.wait_ge(attn_ready, n)
                dve.wait_ge(stored[p % 2], 16 * CREDIT + 16 * (2 * b + p // 2))
                for t in range(2):
                    last = nc.vector.scalar_tensor_tensor(out_sb[:, p % 2, t, :], z[:, p % 2, t, :], z_rstd[:, p, t:t + 1],
                                                          ps_attn[:, D * t:D * (t + 1)], ALU.mult, ALU.add)
                last.then_inc(u_done, 1)

            def stage(b, s):
                dve.wait_ge(chain_pe, NSTAGE * b + s + 1)

            def token_sum(b, q):
                dve.wait_ge(xnT_ready, 4 * b + 4)
                nc.vector.tensor_tensor(tok_sum[:, :], col_sum[q][:, :, 0], col_sum[q][:, :, 1],
                                        ALU.add).then_inc(tok_sum_ready, 1)

            def mean_query(b):
                stage(b, 0)
                nc.vector.tensor_copy(sum_row[:, 0, :], ps_chain[0:1, 0:D])
                nc.vector.tensor_scalar(sum_row[:, 1, :], ps_chain[0:1, 0:D], -1.0 / S, None, ALU.mult)
                nc.vector.scalar_tensor_tensor(q_cols[:, :, 0], ps_chain[:, D:D + DC], 1.0 / S, bq_col,
                                               ALU.mult, ALU.add).then_inc(chain_read, 1)

            def mean_key_value(b):
                stage(b, 1)
                nc.vector.tensor_tensor(k_row[:, :], ps_chain[0:1, 0:D], bk_tokens[:, :], ALU.add)
                nc.vector.scalar_tensor_tensor(v_row[:, :], ps_chain[0:1, D:DC2], 1.0 / S, bv_row,
                                               ALU.mult, ALU.add).then_inc(chain_read, 1)

            def mirror(b):
                stage(b, 2)
                nc.vector.tensor_copy(gram[:, 1, 0:P], ps_chain[:, 0:P]).then_inc(chain_read, 1)

            def head_blocks(b):
                stage(b, 4)
                nc.vector.tensor_tensor(kv[:, :, :], ps_chain[:, 0:DC * P].rearrange("p (c n) -> p c n", c=DC),
                                        head_mask.rearrange("p (o n) -> p o n", o=1).to_broadcast([P, DC, P]),
                                        ALU.mult).then_inc(chain_read, 1)

            def quadratic(b):
                stage(b, 7)
                nc.vector.tensor_tensor(quad[:, :, :], ps_chain[:, :].rearrange("p (c n) -> p c n", c=DC),
                                        map_[:, :, :], ALU.mult).then_inc(chain_read, 1)

            def feature_stats(b):
                stage(b, 8)
                nc.vector.tensor_copy(stat[:, :], ps_chain[:, 0:6]).then_inc(chain_read, 1)

            def spread_in_head(b):
                stage(b, 9)
                n = 4 * b
                nc.vector.tensor_copy(head_avg[:, :], ps_chain[:, 0:DC])
                link(nc.vector.tensor_tensor(dev[:, :], stat[:, 2:6:2], ps_chain[:, 0:DC], ALU.subtract),
                     small_chain, n + 1)
                link(nc.vector.tensor_tensor(dev[:, :], dev[:, :], dev[:, :], ALU.mult), small_chain, n + 2)
                nc.vector.scalar_tensor_tensor(second[:, :], stat[:, 0:DC], 1.0 / S, dev[:, :],
                                               ALU.mult, ALU.add).then_inc(chain_read, 1)

            def head_variance(b):
                stage(b, 10)
                nc.vector.tensor_scalar(head_var[:, :], ps_chain[:, 0:DC], EPS, None, ALU.add)\
                    .then_inc(head_var_ready, 1)

            def group_norm(b):
                dve.wait_ge(head_rstd_ready, b + 1)
                nc.vector.tensor_tensor(gn_shift[:, :], stat[:, 3:6:2], head_avg[:, :], ALU.subtract)
                link(nc.vector.tensor_tensor(gn_scale[:, :], head_rstd[:, :], gnw_col, ALU.mult),
                     small_chain, 4 * b + 3)
                link(nc.vector.tensor_tensor(gn_shift[:, :], gn_shift[:, :], gn_scale[:, :], ALU.mult),
                     small_chain, 4 * b + 4)
                nc.vector.tensor_tensor(gn_shift[:, :], gn_shift[:, :], gnb_col, ALU.add).then_inc(chain_read, 1)
                for c in range(DC):
                    last = nc.vector.tensor_scalar(outw_scaled[:, c, :], outwT_sb[:, c, :], gn_scale[:, c:c + 1],
                                                   None, ALU.mult)
                last.then_inc(scaled_ready, 1)

            def attention_row(b):
                stage(b, 12)
                nc.vector.tensor_tensor(attn_row[:, :], ps_chain[:, 0:D], row_bias[:, :],
                                        ALU.add).then_inc(chain_read, 1)

            def first(nb, half, q):
                for g in range(GROUPS):
                    x_statistics(nb, half, q, g)
                    x_offset(nb, g)
                xn_low(nb, q, 0)
                constants()
                xn_low(nb, q, 1)
                mix(nb, q, 0)
                path_biases()

            def step(b, q, nxt, prev):
                token_sum(b, q)
                mean_query(b)
                choose(b, 0)
                if prev is not None:
                    z_statistics(prev, 1 - q, 2)
                mean_key_value(b)
                mirror(b)
                mask(b, 0, 0)
                if prev is not None:
                    combine(prev, 2)
                if nxt:
                    x_statistics(*nxt, 1 - q, 0)
                mask(b, 0, 1)
                if nxt:
                    x_offset(nxt[0], 0)
                head_blocks(b)
                mix(b, q, 1)
                mask(b, 0, 2)
                if nxt:
                    xn_low(nxt[0], 1 - q, 0)
                mask(b, 0, 3)
                if prev is not None:
                    z_statistics(prev, 1 - q, 3)
                quadratic(b)
                mask(b, 0, 4)
                if prev is not None:
                    combine(prev, 3)
                feature_stats(b)
                spread_in_head(b)
                choose(b, 1)
                head_variance(b)
                if nxt:
                    x_statistics(*nxt, 1 - q, 1)
                group_norm(b)
                if nxt:
                    x_offset(nxt[0], 1)
                z_statistics(b, q, 0)
                mask(b, 1, 0)
                mask(b, 1, 1)
                attention_row(b)
                mask(b, 1, 2)
                combine(b, 0)
                if nxt:
                    xn_low(nxt[0], 1 - q, 1)
                mask(b, 1, 3)
                if nxt:
                    mix(nxt[0], 1 - q, 0)
                z_statistics(b, q, 1)
                mask(b, 1, 4)
                combine(b, 1)

            def tail(b, q):
                for p in (2, 3):
                    z_statistics(b, q, p)
                    combine(b, p)

            batches(dve, first, step, tail)

        @block.tensor
        def _(pe):
            mm = nc.tensor.matmul
            def bias_products():
                pe.wait_ge(prep, 2)
                pe.wait_ge(w2_in, 32)
                for j in range(NJ):
                    r = DM if j == LAST else P
                    last = mm(ps_chain[DM:RK, 0:D], b1_blocks[0:r, j, :], h_flat(hm)[0:r, j * D:(j + 1) * D],
                              start=(j == 0), stop=(j == LAST))
                last.then_inc(bias_prod, 1)

            def transposes(nb, q, g, c):
                pe.wait_ge(xnT_ready, 4 * nb + 2 * g + c)
                for t in range(GROUP):
                    if c == 0:
                        pe.wait_ge(xn_ready, 8 * nb + GROUP * g + t + 1)
                    last = nc.tensor.transpose(ps_t[:, P * t:P * (t + 1)], xn[q][:, GROUP * g + t, P * c:P * (c + 1)],
                                               ident)
                last.then_inc(t_ready, 1)

            def gram_tiles(nb, q, g, half):
                if g == 0 and half == 0:
                    pe.wait_ge(gram_read, nb)
                pe.wait_ge(xn_lo_ready, 4 * nb + 2 * g + half + 1)
                for t in (2 * half, 2 * half + 1):
                    first_one = g == 0 and t == 0
                    for lhs, rhs in ((xn_hi, xn_hi), (xn_hi, xn_lo), (xn_lo, xn_hi)):
                        mm(ps_gram[:, 0:D], lhs[:, t, 0:P], rhs[:, t, :], start=first_one, stop=False,
                           skip_group_check=True)
                        last = mm(ps_gram[:, D:D + P], lhs[:, t, P:D], rhs[:, t, P:D], start=False, stop=False,
                                  skip_group_check=True)
                        first_one = False
                if half == 1:
                    last.then_inc(gram_used, 1)

            def split_mm(ps, parts, started=False, ended=True):
                todo = [(a, r) for lh, ll, rh, rl in parts for a, r in ((lh, rh), (lh, rl), (ll, rh))]
                for i, (a, r) in enumerate(todo):
                    last = mm(ps, a, r, start=(i == 0 and not started), stop=(i == len(todo) - 1 and ended))
                return last

            def hidden(b, g, k):
                j = ORDER[k]
                if k == 0:
                    pe.wait_ge(xm_hi_ready, 4 * b + 2 * g + 2)
                    pe.wait_ge(xm_lo_ready, 4 * b + 2 * g + 2)
                pe.wait_ge(h_copied, CREDIT + 10 * b + NJ * g + k - (1 if NJ * g + k else 0))
                cols_j = slice(P * j, P * (j + 1))
                split_mm(ps_h[(NJ * g + k) % 2][:, :],
                         [(w1_hi[:, c, cols_j], w1_lo[:, c, cols_j], xm_hi[:, g, c, :], xm_lo[:, g, c, :])
                          for c in range(DC)]).then_inc(h_ready, 1)

            def scores(b, g):
                pe.wait_ge(router_hidden, 2 * b + g + 1)
                pe.wait_ge(masked, CREDIT + 10 * b + NJ * g)
                for t in range(GROUP):
                    last = mm(ps_mask[:, E * t:E * (t + 1)], h_sb[DM:P, 0, P * t:P * (t + 1)], wo2_sb[DM:P, :],
                              start=True, stop=True)
                last.then_inc(scores_ready, 1)

            def route(b, g):
                pe.wait_ge(onehot_ready, 2 * b + g + 1)
                for t in range(GROUP):
                    last = mm(ps_mask[DM:RK, P * t:P * (t + 1)], onehot[:, t, :], ident_bf[:, :], start=True, stop=True)
                last.then_inc(route_ready, 1)

            def mask(b, g, k):
                j = ORDER[k]
                if k == 0:
                    pe.wait_ge(route_copied, 2 * b + g + 1)
                else:
                    pe.wait_ge(masked, CREDIT + 10 * b + NJ * g + k)
                mm(ps_mask[:, :], spread[DM:RK, P * j:P * (j + 1)], hm_hi[g][DM:RK, LAST, :], start=True, stop=True)\
                    .then_inc(mask_ready, 1)

            def ffn(b, p, t):
                g = p // 2
                if t == 0:
                    if p % 2 == 0:
                        pe.wait_ge(hm_lo_ready, 10 * b + NJ * (g + 1))
                    pe.wait_ge(z_done, CREDIT + 4 * b + p)
                toks = slice(P * (2 * (p % 2) + t), P * (2 * (p % 2) + t + 1))
                ps, hi, lo = ps_ffn[:, D * t:D * (t + 1)], hm_hi[g], hm_lo[g]
                split_mm(ps, [(hi[:, j, toks], lo[:, j, toks], w2_hi[:, j, :], w2_lo[:, j, :])
                              for j in range(LAST)], ended=False)
                mm(ps, hi[0:RK, LAST, toks], w2_hi[0:RK, LAST, :], start=False, stop=False)
                mm(ps, hi[0:RK, LAST, toks], w2_lo[0:RK, LAST, :], start=False, stop=False)
                last = mm(ps, lo[0:DM, LAST, toks], w2_hi[0:DM, LAST, :], start=False, stop=True)
                if t == 1:
                    last.then_inc(ffn_ready, 1)

            def attention(b, q, p):
                if p == 0:
                    pe.wait_ge(chain_read, CREDIT + NSTAGE * b + 12)
                pe.wait_ge(u_done, CREDIT + 4 * b + p)
                for t in range(2):
                    for c in range(DC):
                        at = 1 + P * (2 * p + t)
                        last = mm(ps_attn[:, D * t:D * (t + 1)], xnT[q][:, c, at:at + P], attn_mat[:, c, :],
                                  start=(c == 0), stop=(c == DC - 1))
                last.then_inc(attn_ready, 1)

            def square(ps, lhs, rhs):
                for m in range(DC):
                    for c in range(DC):
                        last = mm(ps[:, D * m:D * (m + 1)], lhs(c, m), rhs(c), start=(c == 0), stop=(c == DC - 1))
                return last

            def chunk(m):
                return slice(P * m, P * (m + 1))

            def chain(b, q, s):
                if s == 0:
                    pe.wait_ge(tok_sum_ready, b + 1)
                pe.wait_ge(chain_read, CREDIT + NSTAGE * b + s)
                ps = ps_chain
                if s == 0:
                    for c in range(DC):
                        mm(ps[0:1, chunk(c)], tok_sum[:, c:c + 1], ident, start=True, stop=True)
                    for m in range(DC):
                        for c in range(DC):
                            last = mm(ps[:, D + m:D + m + 1], wqkvT_sb[:, c, chunk(m)], tok_sum[:, c:c + 1],
                                      start=(c == 0), stop=(c == DC - 1))
                elif s == 1:
                    for c in range(DC):
                        last = mm(ps[0:1, :], tok_sum[:, c:c + 1], wqkvT_sb[:, c, D:3 * D],
                                  start=(c == 0), stop=(c == DC - 1))
                    last.then_inc(chain_pe, 1)
                    mm(ps_gram[:, 0:D], sum_row[:, 0, 0:P], sum_row[:, 1, :], start=False, stop=False,
                       skip_group_check=True)
                    mm(ps_gram[:, D:D + P], sum_row[:, 0, P:D], sum_row[:, 1, P:D], start=False, stop=True,
                       skip_group_check=True).then_inc(gram_done, 1)
                    return
                elif s == 2:
                    pe.wait_ge(gram_read, b + 1)
                    last = nc.tensor.transpose(ps[:, 0:P], gram[:, 0, P:D], ident)
                elif s == 3:
                    last = square(ps, lambda c, m: gram[:, c, chunk(m)], lambda c: wqkvT_sb[:, c, 2 * D:3 * D])
                elif s == 4:
                    for m in range(DC):
                        for c in range(DC):
                            mm(ps[:, chunk(m)], wqkvT_sb[:, c, D + P * m:D + P * (m + 1)], gram_v[:, c, chunk(m)],
                               start=(c == 0), stop=False)
                        last = mm(ps[:, chunk(m)], k_row[:, chunk(m)], v_row[:, chunk(m)], start=False, stop=True)
                elif s == 5:
                    for c in range(DC):
                        last = mm(ps[:, D * c:D * (c + 1)], kv[:, c, :], wq_sb[:, c, :], start=True, stop=True)
                elif s == 6:
                    for m in range(DC):
                        for c in range(DC):
                            last = mm(ps[:, D * m + P * c:D * m + P * (c + 1)], wq_sb[:, c, chunk(m)], kv[:, c, :],
                                      start=True, stop=True)
                elif s == 7:
                    last = square(ps, lambda c, m: gram[:, c, chunk(m)], lambda c: map_[:, c, :])
                elif s == 8:
                    for m in range(DC):
                        for c in range(DC):
                            mm(ps[:, m:m + 1], quad[:, c, chunk(m)], ones_col, start=(c == 0), stop=(c == DC - 1))
                    for c in range(DC):
                        last = mm(ps[:, 2 + 2 * c:4 + 2 * c], kv[:, c, :], q_cols[:, c, :], start=True, stop=True)
                elif s == 9:
                    last = mm(ps[:, 0:DC], head_mean, stat[:, 2:6:2], start=True, stop=True)
                elif s == 10:
                    last = mm(ps[:, 0:DC], head_mean, second[:, :], start=True, stop=True)
                elif s == 11:
                    pe.wait_ge(scaled_ready, b + 1)
                    last = square(ps, lambda c, m: mapT[:, c, chunk(m)], lambda c: outw_scaled[:, c, :])
                else:
                    for c in range(DC):
                        last = mm(ps[:, 0:D], gn_shift[:, c:c + 1].to_broadcast([P, P]), outwT_sb[:, c, :],
                                  start=(c == 0), stop=(c == DC - 1))
                last.then_inc(chain_pe, 1)

            def first(nb, half, q):
                pe.wait_ge(consts_in, 16)
                for g in range(GROUPS):
                    for c in range(DC):
                        transposes(nb, q, g, c)
                    gram_tiles(nb, q, g, 0)
                    gram_tiles(nb, q, g, 1)
                bias_products()
                pe.wait_ge(prep, 6)

            def step(b, q, nxt, prev):
                hidden(b, 0, 0)
                chain(b, q, 0)
                if prev is not None:
                    ffn(prev, 2, 0)
                scores(b, 0)
                if prev is not None:
                    ffn(prev, 2, 1)
                chain(b, q, 1)
                route(b, 0)
                hidden(b, 0, 1)
                chain(b, q, 2)
                mask(b, 0, 0)
                if prev is not None:
                    attention(prev, 1 - q, 2)
                chain(b, q, 3)
                hidden(b, 0, 2)
                mask(b, 0, 1)
                chain(b, q, 4)
                if prev is not None:
                    ffn(prev, 3, 0)
                mask(b, 0, 2)
                chain(b, q, 5)
                if nxt:
                    transposes(nxt[0], 1 - q, 0, 0)
                hidden(b, 0, 3)
                mask(b, 0, 3)
                chain(b, q, 6)
                if nxt:
                    transposes(nxt[0], 1 - q, 0, 1)
                if prev is not None:
                    ffn(prev, 3, 1)
                chain(b, q, 7)
                if nxt:
                    gram_tiles(nxt[0], 1 - q, 0, 0)
                hidden(b, 0, 4)
                mask(b, 0, 4)
                if prev is not None:
                    attention(prev, 1 - q, 3)
                chain(b, q, 8)
                if nxt:
                    gram_tiles(nxt[0], 1 - q, 0, 1)
                hidden(b, 1, 0)
                chain(b, q, 9)
                ffn(b, 0, 0)
                scores(b, 1)
                chain(b, q, 10)
                ffn(b, 0, 1)
                route(b, 1)
                hidden(b, 1, 1)
                mask(b, 1, 0)
                chain(b, q, 11)
                hidden(b, 1, 2)
                mask(b, 1, 1)
                ffn(b, 1, 0)
                if nxt:
                    transposes(nxt[0], 1 - q, 1, 0)
                chain(b, q, 12)
                mask(b, 1, 2)
                attention(b, q, 0)
                if nxt:
                    transposes(nxt[0], 1 - q, 1, 1)
                hidden(b, 1, 3)
                mask(b, 1, 3)
                if nxt:
                    gram_tiles(nxt[0], 1 - q, 1, 0)
                ffn(b, 1, 1)
                hidden(b, 1, 4)
                mask(b, 1, 4)
                if nxt:
                    gram_tiles(nxt[0], 1 - q, 1, 1)
                attention(b, q, 1)

            def tail(b, q):
                for p in (2, 3):
                    ffn(b, p, 0)
                    ffn(b, p, 1)
                    attention(b, q, p)

            batches(pe, first, step, tail)


def h_flat(t):
    return t[:, :, :].rearrange("p j n -> p (j n)")


def kernel(**inputs):
    import numpy as np
    import concourse.bacc as bacc
    from concourse.bass_utils import run_bass_kernel_spmd

    a = {n.replace("L0_", ""): np.asarray(v) for n, v in inputs.items()}
    f = np.float32
    D = a["attn_x"].shape[2]
    E, DM = a["ffn_b1"].shape
    NJ = (E + 1) * DM // P
    DH = 8

    def as_cols(v):
        return v.reshape(-1, P).T

    b1 = np.zeros((NJ * P,), f)
    b1[:E * DM] = a["ffn_b1"].reshape(-1)
    bo1 = np.zeros((P,), f)
    bo1[DM:] = a["ffn_bo1"]
    cols = np.concatenate([as_cols(a["attn_Wqkv_b"][:D]), as_cols(a["attn_gn_w"]), as_cols(a["attn_gn_b"])]
                          + [as_cols(a["ffn_mix_kernel"][j]) for j in range(3)] + [as_cols(b1), as_cols(bo1)], 1)
    rows = a["attn_Wqkv_b"][None, D:]

    same_head = (np.arange(P)[:, None] // DH == np.arange(P)[None, :] // DH).astype(f)
    feature_path = np.arange(NJ * P) // DM
    path_of = (feature_path[:, None] == np.arange(E)[None, :]).astype(f)
    consts = np.concatenate([np.eye(P, dtype=f), same_head, same_head / DH, np.ones((P, 1), f),
                             np.full((P, 1), -0.5, f), np.tile(np.arange(E, 0, -1, dtype=f), (P, 1)),
                             path_of.reshape(NJ, P, E).transpose(1, 0, 2).reshape(P, NJ * E)], 1)

    arrays = {
        "x": a["attn_x"],
        "wqkv_t": a["attn_Wqkv_w"].T,
        "wq": a["attn_Wqkv_w"][:D],
        "out_wt": a["attn_out_w"].T,
        "w1": np.concatenate([a["ffn_W1"].transpose(1, 0, 2).reshape(D, E * DM), a["ffn_Wo1"]], 1),
        "w2": a["ffn_W2"].reshape(E * DM, D),
        "wo2": a["ffn_Wo2"],
        "b2": a["ffn_b2"],
        "cols": cols,
        "rows": rows,
        "gamma": np.tile(a["ffn_gamma"], (P, 1)),
        "beta": np.tile(a["ffn_beta"], (P, 1)),
        "out_b": np.tile(a["attn_out_b"], (P, 1)),
        "bo2": np.tile(a["ffn_bo2"], (P, 1)),
        "consts": consts,
        "experts": path_of.T,
    }
    nc = bacc.Bacc("TRN2", target_bir_lowering=False, num_devices=1)
    given, args = {}, []
    for name, v in arrays.items():
        given[name] = np.ascontiguousarray(v)
        args.append(nc.dram_tensor(name, v.shape, mybir.dt.from_np(v.dtype), kind="ExternalInput").ap())
    out = nc.dram_tensor("out", a["attn_x"].shape, F32, kind="ExternalOutput").ap()
    block_kernel(nc, *args, out)
    r = run_bass_kernel_spmd(nc, [given], core_ids=[0])
    return r.results[0]["out"]
```

```python
from contextlib import ExitStack

import concourse.bass as bass
from concourse import mybir

ALU = mybir.AluOpType
ACT = mybir.ActivationFunctionType
F32 = mybir.dt.float32
F32R = mybir.dt.float32r
BF16 = mybir.dt.bfloat16
AX_X = mybir.AxisListType.X
EPS = 1e-5

P = 128
GROUP = 4
GROUPS = 2
PAIRS = 4
GT = GROUP * P
SLOTS = 3


def block_kernel(nc, x, wqkv_t, wq, out_wt, w1, w2, wo2, b2, cols, rows, gamma, beta, out_b, bo2, consts, out):
    B, S, D = x.shape
    E = b2.shape[0]
    DM = wo2.shape[0]
    DC = D // P
    NJ = (E + 1) * DM // P
    LAST = NJ - 1
    RK = DM + E
    DC2 = 2 * D
    assert (P, GT * GROUPS, DC, NJ, 2 * DM) == (128, S, 2, 5, P) and B % 2 == 0

    x_dram = x.rearrange("b (p t i) d -> b p i t d", i=P, t=2)
    out_dram = out.rearrange("b (p t i) d -> b p i t d", i=P, t=2)

    ctx = ExitStack()
    with ctx:
        def sb(name, shape, dt=F32):
            return ctx.enter_context(nc.sbuf_tensor(name, shape, dt))

        def sem(name):
            return ctx.enter_context(nc.semaphore(name))

        wqkvT_sb = sb("wqkvT_sb", [P, DC, 3 * D])
        wq_sb = sb("wq_sb", [P, DC, D])
        outwT_sb = sb("outwT_sb", [P, DC, D])
        w1_hi = sb("w1_hi", [P, DC, NJ * P], F32R)
        w1_lo = sb("w1_lo", [P, DC, NJ * P], F32R)
        w2_hi = sb("w2_hi", [P, NJ, D], F32R)
        w2_lo = sb("w2_lo", [P, NJ, D], F32R)
        wo2_sb = sb("wo2_sb", [P, E])
        b2_sb = sb("b2_sb", [P, D])
        path_bias = sb("path_bias", [P, D])
        b1_blocks = sb("b1_blocks", [P, NJ, E])
        cols_sb = sb("cols_sb", [P, cols.shape[1]])
        rows_sb = sb("rows_sb", [1, rows.shape[1]])
        gamma_sb = sb("gamma_sb", [P, D])
        bo2_sb = sb("bo2_sb", [P, E])
        consts_sb = sb("consts_sb", [P, consts.shape[1]])
        ident_bf = sb("ident_bf", [P, P], BF16)
        bk_tokens = sb("bk_tokens", [1, D])
        outb_sb = sb("outb_sb", [P, D])
        row_bias = sb("row_bias", [P, D])
        ident = consts_sb[:, 0:P]
        head_mask = consts_sb[:, P:2 * P]
        head_mean = consts_sb[:, 2 * P:3 * P]
        ones_col = consts_sb[:, 3 * P:3 * P + 1]
        minus_half = consts_sb[:, 3 * P + 1:3 * P + 2]
        rank = consts_sb[:, 3 * P + 2:3 * P + 2 + E]
        feature_rank = consts_sb[:, 3 * P + 2 + E:3 * P + 2 + E + NJ]
        path_of = consts_sb[:, 3 * P + 2 + E + NJ:].rearrange("p (j e) -> p j e", e=E)
        bq_col, gnw_col, gnb_col = cols_sb[:, 0:2], cols_sb[:, 2:4], cols_sb[:, 4:6]
        tap_col = cols_sb[:, 6:12].rearrange("p (j c) -> p j c", c=DC)
        b1_col, bo1_col = cols_sb[:, 12:12 + NJ], cols_sb[:, 12 + NJ:13 + NJ]
        bk_row, bv_row = rows_sb[:, 0:D], rows_sb[:, D:2 * D]

        x_sb = [sb(f"x_sb{q}", [P, 2 * PAIRS, D]) for q in range(2)]
        xn = [sb(f"xn{q}", [P, 2 * PAIRS, D]) for q in range(2)]
        xn_hi = sb("xn_hi", [P, GROUP, D], F32R)
        xn_half = sb("xn_half", [P, GROUP, D], F32R)
        xn_lo = sb("xn_lo", [P, GROUP, D], F32R)
        xnT = [sb(f"xnT{q}", [P, DC, S + 2]) for q in range(2)]
        col_sum = [sb(f"col_sum{q}", [P, DC, GROUPS]) for q in range(2)]
        x_stats = sb("x_stats", [P, GROUPS, GROUP, 6])
        x_mv = sb("x_mv", [P, GROUPS, GROUP, 2])
        x_var = sb("x_var", [P, GROUPS, GROUP])
        x_rstd = sb("x_rstd", [P, GROUPS, GROUP])
        x_shift = sb("x_shift", [P, GROUPS, GROUP])
        xm = sb("xm", [P, GROUPS, DC, GT])
        xm_hi = sb("xm_hi", [P, GROUPS, DC, GT], F32R)
        xm_lo = sb("xm_lo", [P, GROUPS, DC, GT], F32R)
        router_h = sb("router_h", [P, GT])
        hm = sb("hm", [P, SLOTS, GT])
        hm_hi = [sb(f"hm_hi{g}", [P, NJ, GT], F32R) for g in range(GROUPS)]
        hm_lo = [sb(f"hm_lo{g}", [P, NJ, GT], F32R) for g in range(GROUPS)]
        score = sb("score", [P, GROUP, E])
        best = sb("best", [P, GROUP])
        tied = sb("tied", [P, GROUP, E])
        chosen = sb("chosen", [P, GT], BF16)
        choice = sb("choice", [P, GROUP], BF16)
        z = sb("z", [P, 2, 2, D])
        z_stats = sb("z_stats", [P, PAIRS, 2, 6])
        z_mv = sb("z_mv", [P, PAIRS, 2, 2])
        z_var = sb("z_var", [P, PAIRS, 2])
        z_rstd = sb("z_rstd", [P, PAIRS, 2])
        out_sb = sb("out_sb", [P, 2, 2, D])
        tok_sum = sb("tok_sum", [P, DC])
        sum_row = sb("sum_row", [1, 2, D])
        q_cols = sb("q_cols", [P, DC, 2])
        k_row = sb("k_row", [1, D])
        v_row = sb("v_row", [1, D])
        gram = sb("gram", [P, DC, D])
        gram_v = sb("gram_v", [P, DC, D])
        kv = sb("kv", [P, DC, P])
        mapT = sb("mapT", [P, DC, D])
        map_ = sb("map_", [P, DC, D])
        quad = gram_v
        stat = sb("stat", [P, 6])
        head_avg = sb("head_avg", [P, DC])
        dev = sb("dev", [P, DC])
        second = sb("second", [P, DC])
        head_var = sb("head_var", [P, DC])
        head_rstd = sb("head_rstd", [P, DC])
        gn_scale = sb("gn_scale", [P, DC])
        gn_shift = sb("gn_shift", [P, DC])
        outw_scaled = map_
        attn_mat = sb("attn_mat", [P, DC, D])
        attn_row = sb("attn_row", [P, D])

        ps_t, ps_gram, ps_chain, ps_h0, ps_h1, ps_mask, ps_ffn, ps_attn = [
            ctx.enter_context(nc.psum_tensor(n, [P, 512], F32))
            for n in ("ps_t", "ps_gram", "ps_chain", "ps_h0", "ps_h1", "ps_mask", "ps_ffn", "ps_attn")]
        ps_h = [ps_h0, ps_h1]
        w1_stage = h_flat(x_sb[1])[:, 0:DC * NJ * P]
        w2_stage = h_flat(hm)[:, 0:NJ * D]

        consts_in = sem("consts_in")
        weights_in = sem("weights_in")
        w1_in, w2_in = sem("w1_in"), sem("w2_in")
        x_in = [[sem(f"x_in{q}{g}") for g in range(GROUPS)] for q in range(2)]
        prep = sem("prep")
        bias_prod = sem("bias_prod")
        w1_hi_made, w2_hi_made = sem("w1_hi_made"), sem("w2_hi_made")
        stats_chain = sem("stats_chain")
        var_ready = sem("var_ready")
        rstd_ready = sem("rstd_ready")
        shift_ready = sem("shift_ready")
        xn_ready = sem("xn_ready")
        t_ready = sem("t_ready")
        xnT_ready = sem("xnT_ready")
        xn_hi_ready = sem("xn_hi_ready")
        xn_lo_ready = sem("xn_lo_ready")
        xn_half_ready = sem("xn_half_ready")
        gram_used = sem("gram_used")
        gram_done = sem("gram_done")
        gram_read = sem("gram_read")
        center_ready = sem("center_ready")
        left_done = sem("left_done")
        xm_ready = sem("xm_ready")
        xm_hi_ready = sem("xm_hi_ready")
        xm_lo_ready = sem("xm_lo_ready")
        h_ready = sem("h_ready")
        router_hidden = sem("router_hidden")
        scores_ready = sem("scores_ready")
        router_chain = sem("router_chain")
        choice_ready = sem("choice_ready")
        route_ready = sem("route_ready")
        masked = sem("masked")
        chosen_ready = sem("chosen_ready")
        hm_hi_ready = sem("hm_hi_ready")
        hm_lo_ready = sem("hm_lo_ready")
        ffn_ready = sem("ffn_ready")
        z_done = sem("z_done")
        z_chain = sem("z_chain")
        z_var_ready = sem("z_var_ready")
        z_rstd_ready = sem("z_rstd_ready")
        attn_ready = sem("attn_ready")
        u_done = sem("u_done")
        out_ready = sem("out_ready")
        stored = [sem(f"stored{s}") for s in range(2)]
        tok_sum_ready = sem("tok_sum_ready")
        chain_pe = sem("chain_pe")
        chain_read = sem("chain_read")
        small_chain = sem("small_chain")
        head_var_ready = sem("head_var_ready")
        head_rstd_ready = sem("head_rstd_ready")
        scaled_ready = sem("scaled_ready")
        x_biased = sem("x_biased")

        ORDER = [LAST] + list(range(LAST))
        NSTAGE = 13
        WEIGHT_DMAS = 11
        CREDIT = 1

        def batches(eng, first, step, tail):
            first(0, 0, 0)
            step(0, 0, (1, 0), None)
            with eng.Fori(0, B // 2 - 1) as i:
                step(i * 2 + 1, 1, (i * 2 + 2, i + 1), i * 2)
                step(i * 2 + 2, 0, (i * 2 + 3, i + 1), i * 2 + 1)
            step(B - 1, 1, None, B - 2)
            tail(B - 1, 1)

        block = ctx.enter_context(nc.Block())

        @block.sync
        def _(sp):
            def load(nb, q, g):
                for p in (2 * g, 2 * g + 1):
                    sp.dma_start(x_sb[q][:, 2 * p:2 * p + 2, :], x_dram[nb, p]).then_inc(x_in[q][g], 16)

            load(0, 0, 0)
            sp.dma_start(consts_sb[:, :], consts).then_inc(consts_in, 16)
            sp.dma_start(cols_sb[:, :], cols).then_inc(weights_in, 16)
            load(0, 0, 1)
            sp.dma_start(w1_stage.rearrange("p (c n) -> p c n", c=DC),
                         w1.rearrange("(c p) n -> p c n", p=P)).then_inc(w1_in, 16)
            sp.dma_start(w2_stage[:, 0:LAST * D].rearrange("p (j n) -> p j n", n=D),
                         w2[0:LAST * P, :].rearrange("(j p) n -> p j n", p=P)).then_inc(w2_in, 16)
            sp.dma_start(w2_stage[0:DM, LAST * D:NJ * D], w2[LAST * P:E * DM, :]).then_inc(w2_in, 16)
            sp.dma_start(rows_sb[:, :], rows).then_inc(weights_in, 16)
            sp.dma_start(wo2_sb[DM:P, :], wo2).then_inc(weights_in, 16)
            sp.dma_start(b2_sb[DM:RK, :], b2).then_inc(weights_in, 16)
            sp.dma_start(bo2_sb[:, :], bo2).then_inc(weights_in, 16)
            sp.dma_start(gamma_sb[:, :], gamma).then_inc(weights_in, 16)
            sp.dma_start(row_bias[:, :], beta).then_inc(weights_in, 16)
            sp.dma_start(outb_sb[:, :], out_b).then_inc(weights_in, 16)
            sp.dma_start(wqkvT_sb[:, :, :], wqkv_t.rearrange("(c p) n -> p c n", p=P)).then_inc(weights_in, 16)
            sp.dma_start(wq_sb[:, :, :], wq.rearrange("(c p) n -> p c n", p=P)).then_inc(weights_in, 16)
            sp.dma_start(outwT_sb[:, :, :], out_wt.rearrange("(c p) n -> p c n", p=P)).then_inc(weights_in, 16)

            def store(b, p):
                sp.wait_ge(out_ready, CREDIT + PAIRS * b + p + 1)
                sp.dma_start(out_dram[b, p], out_sb[:, p % 2, :, :]).then_inc(stored[p % 2], 16)

            def first(nb, half, q):
                pass

            def step(b, q, nxt, prev):
                if nxt:
                    if prev is not None:
                        sp.wait_ge(out_ready, CREDIT + PAIRS * prev + 2)
                    else:
                        sp.wait_ge(prep, 1)
                    load(nxt[0], 1 - q, 0)
                if prev is not None:
                    store(prev, 2)
                    store(prev, 3)
                if nxt:
                    load(nxt[0], 1 - q, 1)
                store(b, 0)
                store(b, 1)

            def tail(b, q):
                store(b, 2)
                store(b, 3)

            batches(sp, first, step, tail)
            for s in range(2):
                sp.wait_ge(stored[s], 16 * (CREDIT + 2 * B))

        @block.gpsimd
        def _(pool):
            pool.wait_ge(consts_in, 16)

            def x_pow(nb, g):
                pool.wait_ge(var_ready, 2 * nb + g + 1)
                nc.gpsimd.tensor_tensor(x_rstd[:, g, :], x_var[:, g, :],
                                        minus_half.to_broadcast([P, GROUP]), ALU.pow).then_inc(rstd_ready, 1)

            def normalise(nb, q, g):
                pool.wait_ge(shift_ready, 2 * nb + g + 1)
                pool.nop(nofuse=True)
                for t in range(GROUP):
                    nc.gpsimd.tensor_scalar(xn[q][:, GROUP * g + t, :], x_sb[q][:, GROUP * g + t, :],
                                            x_rstd[:, g, t:t + 1], x_shift[:, g, t:t + 1],
                                            ALU.mult, ALU.add).then_inc(xn_ready, 1)

            def mixed_low(b, g):
                for c in range(DC):
                    pool.wait_ge(xm_hi_ready, 4 * b + 2 * g + c + 1)
                    nc.gpsimd.tensor_tensor(xm_lo[:, g, c, :], xm[:, g, c, :], xm_hi[:, g, c, :].bitcast(F32),
                                            ALU.subtract).then_inc(xm_lo_ready, 1)

            def hidden_low(b, g, k):
                j = ORDER[k]
                r = DM if j == LAST else P
                pool.wait_ge(hm_hi_ready, 10 * b + NJ * g + k + 1)
                nc.gpsimd.tensor_tensor(hm_lo[g][0:r, j, :], hm[0:r, k % SLOTS, :], hm_hi[g][0:r, j, :].bitcast(F32),
                                        ALU.subtract).then_inc(hm_lo_ready, 1)

            def z_pow(b, p):
                pool.wait_ge(z_var_ready, 4 * b + p + 1)
                nc.gpsimd.tensor_tensor(z_rstd[:, p, :], z_var[:, p, :], minus_half.to_broadcast([P, 2]),
                                        ALU.pow).then_inc(z_rstd_ready, 1)

            def bias_x(b, q, p):
                pool.wait_ge(chain_read, CREDIT + NSTAGE * (b + 1))
                nc.gpsimd.tensor_tensor(x_sb[q][:, 2 * p:2 * p + 2, :], x_sb[q][:, 2 * p:2 * p + 2, :],
                                        attn_row[:, :].rearrange("p (o n) -> p o n", o=1).to_broadcast([P, 2, D]),
                                        ALU.add).then_inc(x_biased, 1)

            def final(b, q, p):
                pool.wait_ge(x_biased, 4 * b + p + 1)
                pool.wait_ge(u_done, CREDIT + 4 * b + p + 1)
                nc.gpsimd.tensor_tensor(out_sb[:, p % 2, :, :], out_sb[:, p % 2, :, :],
                                        x_sb[q][:, 2 * p:2 * p + 2, :], ALU.add).then_inc(out_ready, 1)

            def head_pow(b):
                pool.wait_ge(head_var_ready, b + 1)
                nc.gpsimd.tensor_tensor(head_rstd[:, :], head_var[:, :], minus_half.to_broadcast([P, DC]),
                                        ALU.pow).then_inc(head_rstd_ready, 1)

            def first(nb, half, q):
                for g in range(GROUPS):
                    x_pow(nb, g)
                    normalise(nb, q, g)
                mixed_low(nb, 0)

            def step(b, q, nxt, prev):
                mixed_low(b, 1)
                if prev is not None:
                    bias_x(prev, 1 - q, 2)
                    bias_x(prev, 1 - q, 3)
                if nxt:
                    x_pow(nxt[0], 0)
                if prev is not None:
                    z_pow(prev, 2)
                if nxt:
                    normalise(nxt[0], 1 - q, 0)
                if prev is not None:
                    final(prev, 1 - q, 2)
                    z_pow(prev, 3)
                hidden_low(b, 0, 0)
                hidden_low(b, 0, 1)
                if prev is not None:
                    final(prev, 1 - q, 3)
                hidden_low(b, 0, 2)
                hidden_low(b, 0, 3)
                hidden_low(b, 0, 4)
                if nxt:
                    x_pow(nxt[0], 1)
                    normalise(nxt[0], 1 - q, 1)
                z_pow(b, 0)
                head_pow(b)
                hidden_low(b, 1, 0)
                hidden_low(b, 1, 1)
                hidden_low(b, 1, 2)
                if nxt:
                    mixed_low(nxt[0], 0)
                bias_x(b, q, 0)
                z_pow(b, 1)
                bias_x(b, q, 1)
                hidden_low(b, 1, 3)
                hidden_low(b, 1, 4)
                final(b, q, 0)
                final(b, q, 1)

            def tail(b, q):
                for p in (2, 3):
                    z_pow(b, p)
                    bias_x(b, q, p)
                    final(b, q, p)

            batches(pool, first, step, tail)

        @block.scalar
        def _(act):
            def w1_high():
                act.wait_ge(w1_in, 16)
                nc.scalar.activation(w1_hi[:, :, :], w1_stage.rearrange("p (c n) -> p c n", c=DC),
                                     ACT.Copy).then_inc(w1_hi_made, 1)

            def w2_high():
                act.wait_ge(w2_in, 32)
                nc.scalar.activation(w2_hi[:, 0:LAST, :], w2_stage[:, 0:LAST * D].rearrange("p (j n) -> p j n", n=D),
                                     ACT.Copy)
                nc.scalar.activation(w2_hi[0:DM, LAST, :], w2_stage[0:DM, LAST * D:NJ * D],
                                     ACT.Copy).then_inc(w2_hi_made, 1)

            def xn_high(nb, q, g, half):
                if half == 0 and not (isinstance(nb, int) and nb == 0 and g == 0):
                    act.wait_ge(gram_used, 2 * nb + g)
                act.wait_ge(xn_ready, 8 * nb + GROUP * g + 2 * half + 2)
                tiles, own = slice(2 * half, 2 * half + 2), slice(GROUP * g + 2 * half, GROUP * g + 2 * half + 2)
                nc.scalar.activation(xn_hi[:, tiles, :], xn[q][:, own, :], ACT.Copy).then_inc(xn_hi_ready, 1)
                nc.scalar.activation(xn_half[:, tiles, :], xn[q][:, own, :], ACT.Copy,
                                     scale=0.5).then_inc(xn_half_ready, 1)

            def transposed(nb, q, g, c):
                act.wait_ge(t_ready, 4 * nb + 2 * g + c + 1)
                nc.scalar.activation(xnT[q][:, c, 1 + GT * g:1 + GT * (g + 1)], ps_t[:, :], ACT.Copy,
                                     accum_out=col_sum[q][:, c, g:g + 1]).then_inc(xnT_ready, 1)

            def center(b, q, g):
                act.wait_ge(xnT_ready, 4 * b + 4)
                for c in range(DC):
                    nc.scalar.activation(xm[:, g, c, :], xnT[q][:, c, 1 + GT * g:1 + GT * (g + 1)], ACT.Copy,
                                         scale=tap_col[:, 1, c:c + 1]).then_inc(center_ready, 1)

            def mixed_high(b, g):
                for c in range(DC):
                    act.wait_ge(xm_ready, 4 * b + 2 * g + c + 1)
                    nc.scalar.activation(xm_hi[:, g, c, :], xm[:, g, c, :], ACT.Copy).then_inc(xm_hi_ready, 1)

            def router(b, g):
                act.wait_ge(h_ready, 10 * b + NJ * g + 1)
                nc.scalar.activation(router_h[DM:P, :], ps_h[(NJ * g) % 2][DM:P, :], ACT.Tanh,
                                     bias=bo1_col[DM:P, :]).then_inc(router_hidden, 1)

            def choices(b, g):
                act.wait_ge(route_ready, 2 * b + g + 1)
                nc.scalar.activation(chosen[:, :], ps_mask[:, :], ACT.Copy).then_inc(chosen_ready, 1)

            def hidden_high(b, g, k):
                j = ORDER[k]
                r = DM if j == LAST else P
                act.wait_ge(masked, CREDIT + 10 * b + NJ * g + k + 1)
                nc.scalar.activation(hm_hi[g][0:r, j, :], hm[0:r, k % SLOTS, :], ACT.Copy).then_inc(hm_hi_ready, 1)

            def read_stage(b, s, dst):
                act.wait_ge(chain_pe, NSTAGE * b + s + 1)
                nc.scalar.activation(dst, ps_chain[:, :].rearrange("p (c n) -> p c n", c=DC),
                                     ACT.Copy).then_inc(chain_read, 1)

            def read_gram(b):
                act.wait_ge(gram_done, b + 1)
                nc.scalar.activation(gram[:, :, :], ps_gram[:, :].rearrange("p (c n) -> p c n", c=DC),
                                     ACT.Copy).then_inc(gram_read, 1)

            def first(nb, half, q):
                for g in range(GROUPS):
                    for c in range(DC):
                        transposed(nb, q, g, c)
                    if g == 0:
                        w1_high()
                act.wait_ge(weights_in, 16 * WEIGHT_DMAS)
                center(nb, q, 0)
                for half in range(2):
                    xn_high(nb, q, 0, half)
                mixed_high(nb, 0)
                w2_high()
                for half in range(2):
                    xn_high(nb, q, 1, half)

            def step(b, q, nxt, prev):
                router(b, 0)
                center(b, q, 1)
                read_gram(b)
                mixed_high(b, 1)
                read_stage(b, 3, gram_v[:, :, :])
                choices(b, 0)
                hidden_high(b, 0, 0)
                hidden_high(b, 0, 1)
                if nxt:
                    xn_high(nxt[0], 1 - q, 0, 0)
                read_stage(b, 5, mapT[:, :, :])
                hidden_high(b, 0, 2)
                read_stage(b, 6, map_[:, :, :])
                hidden_high(b, 0, 3)
                if nxt:
                    xn_high(nxt[0], 1 - q, 0, 1)
                hidden_high(b, 0, 4)
                router(b, 1)
                if nxt:
                    transposed(nxt[0], 1 - q, 0, 0)
                choices(b, 1)
                if nxt:
                    transposed(nxt[0], 1 - q, 0, 1)
                    xn_high(nxt[0], 1 - q, 1, 0)
                    transposed(nxt[0], 1 - q, 1, 0)
                hidden_high(b, 1, 0)
                if nxt:
                    xn_high(nxt[0], 1 - q, 1, 1)
                hidden_high(b, 1, 1)
                if nxt:
                    transposed(nxt[0], 1 - q, 1, 1)
                    center(nxt[0], 1 - q, 0)
                read_stage(b, 11, attn_mat[:, :, :])
                hidden_high(b, 1, 2)
                if nxt:
                    mixed_high(nxt[0], 0)
                hidden_high(b, 1, 3)
                hidden_high(b, 1, 4)

            def tail(b, q):
                pass

            batches(act, first, step, tail)

        @block.vector
        def _(dve):
            def link(ins, s, value):
                ins.then_inc(s, 1)
                dve.wait_ge(s, value)

            free = [(masked, 1), (z_done, 1), (u_done, 1), (chain_read, 1), (out_ready, 1),
                    (stored[0], 16), (stored[1], 16)]
            edges = [xnT[q][:, c, at:at + 1] for q in range(2) for c in range(DC) for at in (0, S + 1)]
            nc.vector.memset(edges.pop(), 0.0)
            for edge, (s, credit) in zip(edges, free):
                nc.vector.memset(edge, 0.0).then_inc(s, credit)

            def w1_low():
                dve.wait_ge(w1_hi_made, 1)
                nc.vector.tensor_tensor(w1_lo[:, :, :], w1_stage.rearrange("p (c n) -> p c n", c=DC),
                                        w1_hi[:, :, :].bitcast(F32), ALU.subtract).then_inc(prep, 1)

            def constants():
                dve.wait_ge(weights_in, 16 * WEIGHT_DMAS)
                dve.wait_ge(consts_in, 16)
                nc.vector.tensor_copy(ident_bf[:, :], ident)
                for c in range(DC):
                    nc.vector.tensor_copy(q_cols[:, c, 1:2], bq_col[:, c:c + 1])
                nc.vector.tensor_scalar(bk_tokens[:, :], bk_row, float(S), None, ALU.mult)
                nc.vector.tensor_tensor(row_bias[:, :], row_bias[:, :], outb_sb[:, :], ALU.add)
                nc.vector.tensor_tensor(b1_blocks[:, :, :], path_of,
                                        b1_col.rearrange("p (j a) -> p j a", a=1).to_broadcast([P, NJ, E]),
                                        ALU.mult).then_inc(prep, 1)

            def w2_low():
                dve.wait_ge(w2_hi_made, 1)
                nc.vector.tensor_tensor(w2_lo[:, 0:LAST, :], w2_stage[:, 0:LAST * D].rearrange("p (j n) -> p j n", n=D),
                                        w2_hi[:, 0:LAST, :].bitcast(F32), ALU.subtract)
                nc.vector.tensor_tensor(w2_lo[0:DM, LAST, :], w2_stage[0:DM, LAST * D:NJ * D],
                                        w2_hi[0:DM, LAST, :].bitcast(F32), ALU.subtract).then_inc(prep, 1)

            def path_biases():
                dve.wait_ge(bias_prod, 1)
                link(nc.vector.tensor_tensor(path_bias[DM:RK, :], ps_chain[DM:RK, 0:D], b2_sb[DM:RK, :], ALU.add),
                     prep, 4)
                link(nc.vector.tensor_copy(w2_hi[DM:RK, LAST, :], path_bias[DM:RK, :]), prep, 5)
                nc.vector.tensor_tensor(w2_lo[DM:RK, LAST, :], path_bias[DM:RK, :],
                                        w2_hi[DM:RK, LAST, :].bitcast(F32), ALU.subtract).then_inc(prep, 1)

            def x_statistics(nb, half, q, g):
                dve.wait_ge(x_in[q][g], 32 * (half + 1))
                for t in range(GROUP):
                    last = nc.vector.bn_stats(x_stats[:, g, t, :], x_sb[q][:, GROUP * g + t, :])
                link(last, stats_chain, 4 * nb + 2 * g + 1)
                dve.nop(nofuse=True)
                for t in range(GROUP):
                    last = nc.vector.bn_aggr(x_mv[:, g, t, :], x_stats[:, g, t, :])
                link(last, stats_chain, 4 * nb + 2 * g + 2)
                nc.vector.tensor_scalar(x_var[:, g, :], x_mv[:, g, :, 1], EPS, None, ALU.add).then_inc(var_ready, 1)

            def xn_low(nb, q, g, half):
                dve.wait_ge(xn_hi_ready, 4 * nb + 2 * g + half + 1)
                tiles, own = slice(2 * half, 2 * half + 2), slice(GROUP * g + 2 * half, GROUP * g + 2 * half + 2)
                nc.vector.tensor_tensor(xn_lo[:, tiles, :], xn[q][:, own, :], xn_hi[:, tiles, :].bitcast(F32),
                                        ALU.subtract).then_inc(xn_lo_ready, 1)

            def x_offset(nb, g):
                dve.wait_ge(rstd_ready, 2 * nb + g + 1)
                nc.vector.scalar_tensor_tensor(x_shift[:, g, :], x_mv[:, g, :, 0], -1.0, x_rstd[:, g, :],
                                               ALU.mult, ALU.mult).then_inc(shift_ready, 1)

            def mix(b, q, g):
                for c in range(DC):
                    n = 4 * b + 2 * g + c + 1
                    dve.wait_ge(center_ready, n)
                    link(nc.vector.scalar_tensor_tensor(xm[:, g, c, :], xnT[q][:, c, GT * g:GT * (g + 1)],
                                                        tap_col[:, 0, c:c + 1], xm[:, g, c, :],
                                                        ALU.mult, ALU.add), left_done, n)
                    nc.vector.scalar_tensor_tensor(xm[:, g, c, :], xnT[q][:, c, 2 + GT * g:2 + GT * (g + 1)],
                                                   tap_col[:, 2, c:c + 1], xm[:, g, c, :],
                                                   ALU.mult, ALU.add).then_inc(xm_ready, 1)

            def choose(b, g):
                n = 8 * b + 4 * g
                dve.wait_ge(scores_ready, 2 * b + g + 1)

                link(nc.vector.tensor_tensor(score[:, :, :], ps_mask[:, 0:GROUP * E].rearrange("p (t e) -> p t e", e=E),
                                             bo2_sb[:, :].rearrange("p (o e) -> p o e", o=1).to_broadcast([P, GROUP, E]),
                                             ALU.add), router_chain, n + 1)
                link(nc.vector.tensor_reduce(best[:, :], score[:, :, :], AX_X, ALU.max), router_chain, n + 2)
                link(nc.vector.tensor_tensor(tied[:, :, :], score[:, :, :],
                                             best[:, :].rearrange("p (t o) -> p t o", o=1).to_broadcast([P, GROUP, E]),
                                             ALU.is_equal), router_chain, n + 3)
                link(nc.vector.tensor_tensor(tied[:, :, :], tied[:, :, :],
                                             rank.rearrange("p (o e) -> p o e", o=1).to_broadcast([P, GROUP, E]),
                                             ALU.mult), router_chain, n + 4)
                nc.vector.tensor_reduce(choice[:, :], tied[:, :, :], AX_X, ALU.max).then_inc(choice_ready, 1)

            def path_rows(b, g):
                dve.wait_ge(chosen_ready, 2 * b + g + 1)
                nc.vector.tensor_scalar(hm_hi[g][DM:RK, LAST, :], chosen[DM:RK, :], feature_rank[DM:RK, LAST:NJ],
                                        None, ALU.is_equal)

            def mask(b, g, k):
                n = 10 * b + NJ * g + k + 1
                j = ORDER[k]
                r = DM if j == LAST else P
                dve.wait_ge(h_ready, n)
                before = NJ - SLOTS if k < NJ - SLOTS else SLOTS
                if not (isinstance(n, int) and n <= SLOTS):
                    dve.wait_ge(hm_lo_ready, n - before)
                nc.vector.scalar_tensor_tensor(hm[0:r, k % SLOTS, :], chosen[0:r, :], feature_rank[0:r, j:j + 1],
                                               ps_h[(NJ * g + k) % 2][0:r, :], ALU.is_equal,
                                               ALU.mult).then_inc(masked, 1)

            def z_statistics(b, q, p):
                n = 4 * b + p + 1
                dve.wait_ge(ffn_ready, n)
                link(nc.vector.tensor_tensor(z[:, p % 2, :, :], ps_ffn[:, :].rearrange("p (t n) -> p t n", t=2),
                                             xn[q][:, 2 * p:2 * p + 2, :], ALU.add), z_done, CREDIT + n)
                for t in range(2):
                    last = nc.vector.bn_stats(z_stats[:, p, t, :], z[:, p % 2, t, :])
                link(last, z_chain, 3 * n - 2)
                dve.nop(nofuse=True)
                for t in range(2):
                    last = nc.vector.bn_aggr(z_mv[:, p, t, :], z_stats[:, p, t, :])
                link(last, z_chain, 3 * n - 1)
                nc.vector.tensor_scalar(z_var[:, p, :], z_mv[:, p, :, 1], EPS, None, ALU.add).then_inc(z_var_ready, 1)
                for t in range(2):
                    last = nc.vector.scalar_tensor_tensor(z[:, p % 2, t, :], z[:, p % 2, t, :], z_mv[:, p, t, 0:1],
                                                          gamma_sb[:, :], ALU.subtract, ALU.mult)
                link(last, z_chain, 3 * n)

            def combine(b, p):
                n = 4 * b + p + 1
                dve.wait_ge(z_rstd_ready, n)
                dve.wait_ge(attn_ready, n)
                dve.wait_ge(stored[p % 2], 16 * CREDIT + 16 * (2 * b + p // 2))
                for t in range(2):
                    last = nc.vector.scalar_tensor_tensor(out_sb[:, p % 2, t, :], z[:, p % 2, t, :], z_rstd[:, p, t:t + 1],
                                                          ps_attn[:, D * t:D * (t + 1)], ALU.mult, ALU.add)
                last.then_inc(u_done, 1)

            def stage(b, s):
                dve.wait_ge(chain_pe, NSTAGE * b + s + 1)

            def token_sum(b, q):
                dve.wait_ge(xnT_ready, 4 * b + 4)
                nc.vector.tensor_tensor(tok_sum[:, :], col_sum[q][:, :, 0], col_sum[q][:, :, 1],
                                        ALU.add).then_inc(tok_sum_ready, 1)

            def mean_query(b):
                stage(b, 0)
                nc.vector.tensor_copy(sum_row[:, 0, :], ps_chain[0:1, 0:D])
                nc.vector.tensor_scalar(sum_row[:, 1, :], ps_chain[0:1, 0:D], -0.5 / S, None, ALU.mult)
                nc.vector.scalar_tensor_tensor(q_cols[:, :, 0], ps_chain[:, D:D + DC], 1.0 / S, bq_col,
                                               ALU.mult, ALU.add).then_inc(chain_read, 1)

            def mean_key_value(b):
                stage(b, 1)
                nc.vector.tensor_tensor(k_row[:, :], ps_chain[0:1, 0:D], bk_tokens[:, :], ALU.add)
                nc.vector.scalar_tensor_tensor(v_row[:, :], ps_chain[0:1, D:DC2], 1.0 / S, bv_row,
                                               ALU.mult, ALU.add).then_inc(chain_read, 1)

            def symmetric(b):
                stage(b, 2)
                dve.wait_ge(gram_read, b + 1)
                nc.vector.tensor_tensor(gram[:, :, :], gram[:, :, :], ps_chain[:, :].rearrange("p (c n) -> p c n", c=DC),
                                        ALU.add).then_inc(chain_read, 1)

            def head_blocks(b):
                stage(b, 4)
                nc.vector.tensor_tensor(kv[:, :, :], ps_chain[:, 0:DC * P].rearrange("p (c n) -> p c n", c=DC),
                                        head_mask.rearrange("p (o n) -> p o n", o=1).to_broadcast([P, DC, P]),
                                        ALU.mult).then_inc(chain_read, 1)

            def quadratic(b):
                stage(b, 7)
                for c in range(DC):
                    last = nc.vector.scalar_tensor_tensor(quad[:, c, :], ps_chain[:, D * c:D * (c + 1)], 1.0,
                                                          mapT[:, c, :], ALU.mult, ALU.mult,
                                                          accum_out=stat[:, c:c + 1])
                last.then_inc(chain_read, 1)

            def feature_stats(b):
                stage(b, 8)
                nc.vector.tensor_copy(stat[:, DC:6], ps_chain[:, 0:4]).then_inc(chain_read, 1)

            def spread_in_head(b):
                stage(b, 9)
                n = 4 * b
                nc.vector.tensor_copy(head_avg[:, :], ps_chain[:, 0:DC])
                link(nc.vector.tensor_tensor(dev[:, :], stat[:, 2:6:2], ps_chain[:, 0:DC], ALU.subtract),
                     small_chain, n + 1)
                link(nc.vector.tensor_tensor(dev[:, :], dev[:, :], dev[:, :], ALU.mult), small_chain, n + 2)
                nc.vector.scalar_tensor_tensor(second[:, :], stat[:, 0:DC], 1.0 / S, dev[:, :],
                                               ALU.mult, ALU.add).then_inc(chain_read, 1)

            def head_variance(b):
                stage(b, 10)
                nc.vector.tensor_scalar(head_var[:, :], ps_chain[:, 0:DC], EPS, None, ALU.add)\
                    .then_inc(head_var_ready, 1)

            def group_norm(b):
                dve.wait_ge(head_rstd_ready, b + 1)
                nc.vector.tensor_tensor(gn_shift[:, :], stat[:, 3:6:2], head_avg[:, :], ALU.subtract)
                link(nc.vector.tensor_tensor(gn_scale[:, :], head_rstd[:, :], gnw_col, ALU.mult),
                     small_chain, 4 * b + 3)
                link(nc.vector.tensor_tensor(gn_shift[:, :], gn_shift[:, :], gn_scale[:, :], ALU.mult),
                     small_chain, 4 * b + 4)
                nc.vector.tensor_tensor(gn_shift[:, :], gn_shift[:, :], gnb_col, ALU.add).then_inc(chain_read, 1)
                for c in range(DC):
                    last = nc.vector.tensor_scalar(outw_scaled[:, c, :], outwT_sb[:, c, :], gn_scale[:, c:c + 1],
                                                   None, ALU.mult)
                last.then_inc(scaled_ready, 1)

            def attention_row(b):
                stage(b, 12)
                if not isinstance(b, int) or b > 0:
                    dve.wait_ge(x_biased, PAIRS * b)
                nc.vector.tensor_tensor(attn_row[:, :], ps_chain[:, 0:D], row_bias[:, :],
                                        ALU.add).then_inc(chain_read, 1)

            def first(nb, half, q):
                for g in range(GROUPS):
                    x_statistics(nb, half, q, g)
                    x_offset(nb, g)
                w1_low()
                constants()
                mix(nb, q, 0)
                token_sum(nb, q)
                for half in range(2):
                    xn_low(nb, q, 0, half)
                w2_low()
                path_biases()
                for half in range(2):
                    xn_low(nb, q, 1, half)

            def step(b, q, nxt, prev):
                mean_query(b)
                mix(b, q, 1)
                mean_key_value(b)
                choose(b, 0)
                symmetric(b)
                if nxt:
                    x_statistics(*nxt, 1 - q, 0)
                if prev is not None:
                    z_statistics(prev, 1 - q, 2)
                if nxt:
                    x_offset(nxt[0], 0)
                path_rows(b, 0)
                mask(b, 0, 0)
                if prev is not None:
                    combine(prev, 2)
                head_blocks(b)
                mask(b, 0, 1)
                if prev is not None:
                    z_statistics(prev, 1 - q, 3)
                mask(b, 0, 2)
                if prev is not None:
                    combine(prev, 3)
                mask(b, 0, 3)
                if nxt:
                    xn_low(nxt[0], 1 - q, 0, 0)
                mask(b, 0, 4)
                if nxt:
                    xn_low(nxt[0], 1 - q, 0, 1)
                quadratic(b)
                if nxt:
                    x_statistics(*nxt, 1 - q, 1)
                feature_stats(b)
                choose(b, 1)
                if nxt:
                    x_offset(nxt[0], 1)
                spread_in_head(b)
                z_statistics(b, q, 0)
                head_variance(b)
                path_rows(b, 1)
                mask(b, 1, 0)
                mask(b, 1, 1)
                group_norm(b)
                if nxt:
                    xn_low(nxt[0], 1 - q, 1, 0)
                mask(b, 1, 2)
                if nxt:
                    xn_low(nxt[0], 1 - q, 1, 1)
                    mix(nxt[0], 1 - q, 0)
                mask(b, 1, 3)
                if nxt:
                    token_sum(nxt[0], 1 - q)
                combine(b, 0)
                attention_row(b)
                z_statistics(b, q, 1)
                mask(b, 1, 4)
                combine(b, 1)

            def tail(b, q):
                for p in (2, 3):
                    z_statistics(b, q, p)
                    combine(b, p)

            batches(dve, first, step, tail)

        @block.tensor
        def _(pe):
            mm = nc.tensor.matmul
            def bias_products():
                pe.wait_ge(prep, 2)
                pe.wait_ge(w2_in, 32)
                for j in range(NJ):
                    r = DM if j == LAST else P
                    last = mm(ps_chain[DM:RK, 0:D], b1_blocks[0:r, j, :], w2_stage[0:r, j * D:(j + 1) * D],
                              start=(j == 0), stop=(j == LAST))
                last.then_inc(bias_prod, 1)

            def transposes(nb, q, g, c):
                pe.wait_ge(xnT_ready, 4 * nb + 2 * g + c)
                for t in range(GROUP):
                    if c == 0:
                        pe.wait_ge(xn_ready, 8 * nb + GROUP * g + t + 1)
                    last = nc.tensor.transpose(ps_t[:, P * t:P * (t + 1)], xn[q][:, GROUP * g + t, P * c:P * (c + 1)],
                                               ident)
                last.then_inc(t_ready, 1)

            def gram_tiles(nb, q, g, half):
                if g == 0 and half == 0:
                    pe.wait_ge(gram_read, nb)
                pe.wait_ge(xn_half_ready, 4 * nb + 2 * g + half + 1)
                pe.wait_ge(xn_lo_ready, 4 * nb + 2 * g + half + 1)
                for t in (2 * half, 2 * half + 1):
                    for c in range(DC):
                        for rhs in (xn_half, xn_lo):
                            last = mm(ps_gram[:, D * c:D * (c + 1)], xn_hi[:, t, P * c:P * (c + 1)], rhs[:, t, :],
                                      start=(g == 0 and t == 0 and c == 0 and rhs is xn_half), stop=False,
                                      skip_group_check=True)
                if half == 1:
                    last.then_inc(gram_used, 1)

            def split_mm(ps, parts, started=False, ended=True):
                todo = [(a, r) for lh, ll, rh, rl in parts for a, r in ((lh, rh), (lh, rl), (ll, rh))]
                for i, (a, r) in enumerate(todo):
                    last = mm(ps, a, r, start=(i == 0 and not started), stop=(i == len(todo) - 1 and ended))
                return last

            def hidden(b, g, k):
                j = ORDER[k]
                if k == 0:
                    pe.wait_ge(xm_hi_ready, 4 * b + 2 * g + 2)
                    pe.wait_ge(xm_lo_ready, 4 * b + 2 * g + 2)
                pe.wait_ge(masked, CREDIT + 10 * b + NJ * g + k - (1 if NJ * g + k else 0))
                cols_j = slice(P * j, P * (j + 1))
                split_mm(ps_h[(NJ * g + k) % 2][:, :],
                         [(w1_hi[:, c, cols_j], w1_lo[:, c, cols_j], xm_hi[:, g, c, :], xm_lo[:, g, c, :])
                          for c in range(DC)]).then_inc(h_ready, 1)

            def scores(b, g):
                pe.wait_ge(router_hidden, 2 * b + g + 1)
                pe.wait_ge(chosen_ready, 2 * b + g)
                for t in range(GROUP):
                    last = mm(ps_mask[:, E * t:E * (t + 1)], router_h[DM:P, P * t:P * (t + 1)], wo2_sb[DM:P, :],
                              start=True, stop=True)
                last.then_inc(scores_ready, 1)

            def route(b, g):
                pe.wait_ge(choice_ready, 2 * b + g + 1)
                for t in range(GROUP):
                    last = mm(ps_mask[:, P * t:P * (t + 1)], choice[:, t:t + 1].to_broadcast([P, P]), ident_bf[:, :],
                              start=True, stop=True)
                last.then_inc(route_ready, 1)

            def ffn(b, p, t):
                g = p // 2
                if t == 0:
                    if p % 2 == 0:
                        pe.wait_ge(hm_lo_ready, 10 * b + NJ * (g + 1))
                    pe.wait_ge(z_done, CREDIT + 4 * b + p)
                toks = slice(P * (2 * (p % 2) + t), P * (2 * (p % 2) + t + 1))
                ps, hi, lo = ps_ffn[:, D * t:D * (t + 1)], hm_hi[g], hm_lo[g]
                split_mm(ps, [(hi[:, j, toks], lo[:, j, toks], w2_hi[:, j, :], w2_lo[:, j, :])
                              for j in range(LAST)], ended=False)
                mm(ps, hi[0:RK, LAST, toks], w2_hi[0:RK, LAST, :], start=False, stop=False)
                mm(ps, hi[0:RK, LAST, toks], w2_lo[0:RK, LAST, :], start=False, stop=False)
                last = mm(ps, lo[0:DM, LAST, toks], w2_hi[0:DM, LAST, :], start=False, stop=True)
                if t == 1:
                    last.then_inc(ffn_ready, 1)

            def attention(b, q, p):
                if p == 0:
                    pe.wait_ge(chain_read, CREDIT + NSTAGE * b + 12)
                pe.wait_ge(u_done, CREDIT + 4 * b + p)
                for t in range(2):
                    for c in range(DC):
                        at = 1 + P * (2 * p + t)
                        last = mm(ps_attn[:, D * t:D * (t + 1)], xnT[q][:, c, at:at + P], attn_mat[:, c, :],
                                  start=(c == 0), stop=(c == DC - 1))
                last.then_inc(attn_ready, 1)

            def square(ps, lhs, rhs):
                for m in range(DC):
                    for c in range(DC):
                        last = mm(ps[:, D * m:D * (m + 1)], lhs(c, m), rhs(c), start=(c == 0), stop=(c == DC - 1))
                return last

            def chunk(m):
                return slice(P * m, P * (m + 1))

            def chain(b, q, s):
                if s == 0:
                    pe.wait_ge(tok_sum_ready, b + 1)
                pe.wait_ge(chain_read, CREDIT + NSTAGE * b + s)
                ps = ps_chain
                if s == 0:
                    for c in range(DC):
                        mm(ps[0:1, chunk(c)], tok_sum[:, c:c + 1], ident, start=True, stop=True)
                    for m in range(DC):
                        for c in range(DC):
                            last = mm(ps[:, D + m:D + m + 1], wqkvT_sb[:, c, chunk(m)], tok_sum[:, c:c + 1],
                                      start=(c == 0), stop=(c == DC - 1))
                elif s == 1:
                    for c in range(DC):
                        last = mm(ps[0:1, :], tok_sum[:, c:c + 1], wqkvT_sb[:, c, D:3 * D],
                                  start=(c == 0), stop=(c == DC - 1))
                    last.then_inc(chain_pe, 1)
                    for c in range(DC):
                        last = mm(ps_gram[:, D * c:D * (c + 1)], sum_row[:, 0, chunk(c)], sum_row[:, 1, :], start=False,
                                  stop=(c == DC - 1), skip_group_check=True)
                    last.then_inc(gram_done, 1)
                    return
                elif s == 2:
                    pe.wait_ge(gram_read, b + 1)
                    for m in range(DC):
                        for c in range(DC):
                            last = nc.tensor.transpose(ps[:, D * m + P * c:D * m + P * (c + 1)], gram[:, c, chunk(m)],
                                                       ident)
                elif s == 3:
                    last = square(ps, lambda c, m: gram[:, c, chunk(m)], lambda c: wqkvT_sb[:, c, 2 * D:3 * D])
                elif s == 4:
                    for m in range(DC):
                        for c in range(DC):
                            mm(ps[:, chunk(m)], wqkvT_sb[:, c, D + P * m:D + P * (m + 1)], gram_v[:, c, chunk(m)],
                               start=(c == 0), stop=False)
                        last = mm(ps[:, chunk(m)], k_row[:, chunk(m)], v_row[:, chunk(m)], start=False, stop=True)
                elif s == 5:
                    for c in range(DC):
                        last = mm(ps[:, D * c:D * (c + 1)], kv[:, c, :], wq_sb[:, c, :], start=True, stop=True)
                elif s == 6:
                    for m in range(DC):
                        for c in range(DC):
                            last = mm(ps[:, D * m + P * c:D * m + P * (c + 1)], wq_sb[:, c, chunk(m)], kv[:, c, :],
                                      start=True, stop=True)
                elif s == 7:
                    last = square(ps, lambda c, m: map_[:, c, chunk(m)], lambda c: gram[:, c, :])
                elif s == 8:
                    for c in range(DC):
                        last = mm(ps[:, 2 * c:2 * c + 2], kv[:, c, :], q_cols[:, c, :], start=True, stop=True)
                elif s == 9:
                    last = mm(ps[:, 0:DC], head_mean, stat[:, 2:6:2], start=True, stop=True)
                elif s == 10:
                    last = mm(ps[:, 0:DC], head_mean, second[:, :], start=True, stop=True)
                elif s == 11:
                    pe.wait_ge(scaled_ready, b + 1)
                    last = square(ps, lambda c, m: mapT[:, c, chunk(m)], lambda c: outw_scaled[:, c, :])
                else:
                    for c in range(DC):
                        last = mm(ps[:, 0:D], gn_shift[:, c:c + 1].to_broadcast([P, P]), outwT_sb[:, c, :],
                                  start=(c == 0), stop=(c == DC - 1))
                last.then_inc(chain_pe, 1)

            def first(nb, half, q):
                pe.wait_ge(consts_in, 16)
                for g in range(GROUPS):
                    for c in range(DC):
                        transposes(nb, q, g, c)
                for half in range(2):
                    gram_tiles(nb, q, 0, half)
                bias_products()
                for half in range(2):
                    gram_tiles(nb, q, 1, half)
                pe.wait_ge(prep, 6)

            def step(b, q, nxt, prev):
                chain(b, q, 0)
                hidden(b, 0, 0)
                if prev is not None:
                    attention(prev, 1 - q, 2)
                chain(b, q, 1)
                scores(b, 0)
                if prev is not None:
                    ffn(prev, 2, 0)
                chain(b, q, 2)
                hidden(b, 0, 1)
                if prev is not None:
                    ffn(prev, 2, 1)
                chain(b, q, 3)
                route(b, 0)
                if prev is not None:
                    ffn(prev, 3, 0)
                chain(b, q, 4)
                if prev is not None:
                    ffn(prev, 3, 1)
                hidden(b, 0, 2)
                chain(b, q, 5)
                if prev is not None:
                    attention(prev, 1 - q, 3)
                hidden(b, 0, 3)
                chain(b, q, 6)
                hidden(b, 0, 4)
                hidden(b, 1, 0)
                chain(b, q, 7)
                if nxt:
                    transposes(nxt[0], 1 - q, 0, 0)
                hidden(b, 1, 1)
                scores(b, 1)
                chain(b, q, 8)
                ffn(b, 0, 0)
                chain(b, q, 9)
                ffn(b, 0, 1)
                if nxt:
                    transposes(nxt[0], 1 - q, 0, 1)
                    gram_tiles(nxt[0], 1 - q, 0, 0)
                route(b, 1)
                chain(b, q, 10)
                if nxt:
                    gram_tiles(nxt[0], 1 - q, 0, 1)
                ffn(b, 1, 0)
                if nxt:
                    transposes(nxt[0], 1 - q, 1, 0)
                ffn(b, 1, 1)
                hidden(b, 1, 2)
                if nxt:
                    transposes(nxt[0], 1 - q, 1, 1)
                chain(b, q, 11)
                hidden(b, 1, 3)
                if nxt:
                    gram_tiles(nxt[0], 1 - q, 1, 0)
                attention(b, q, 0)
                chain(b, q, 12)
                if nxt:
                    gram_tiles(nxt[0], 1 - q, 1, 1)
                hidden(b, 1, 4)
                attention(b, q, 1)

            def tail(b, q):
                for p in (2, 3):
                    ffn(b, p, 0)
                    ffn(b, p, 1)
                    attention(b, q, p)

            batches(pe, first, step, tail)


def h_flat(t):
    return t[:, :, :].rearrange("p j n -> p (j n)")


def kernel(**inputs):
    import numpy as np
    import concourse.bacc as bacc
    from concourse.bass_utils import run_bass_kernel_spmd

    a = {n.replace("L0_", ""): np.asarray(v) for n, v in inputs.items()}
    f = np.float32
    D = a["attn_x"].shape[2]
    E, DM = a["ffn_b1"].shape
    NJ = (E + 1) * DM // P
    DH = 8

    def as_cols(v):
        return v.reshape(-1, P).T

    b1 = np.zeros((NJ * P,), f)
    b1[:E * DM] = a["ffn_b1"].reshape(-1)
    bo1 = np.zeros((P,), f)
    bo1[DM:] = a["ffn_bo1"]
    cols = np.concatenate([as_cols(a["attn_Wqkv_b"][:D]), as_cols(a["attn_gn_w"]), as_cols(a["attn_gn_b"])]
                          + [as_cols(a["ffn_mix_kernel"][j]) for j in range(3)] + [as_cols(b1), as_cols(bo1)], 1)
    rows = a["attn_Wqkv_b"][None, D:]

    same_head = (np.arange(P)[:, None] // DH == np.arange(P)[None, :] // DH).astype(f)
    feature_path = np.arange(NJ * P) // DM
    path_of = (feature_path[:, None] == np.arange(E)[None, :]).astype(f)
    feature_rank = (E - feature_path).astype(f)
    feature_rank[E * DM:E * DM + E] = np.arange(E, 0, -1)
    consts = np.concatenate([np.eye(P, dtype=f), same_head, same_head / DH, np.ones((P, 1), f),
                             np.full((P, 1), -0.5, f), np.tile(np.arange(E, 0, -1, dtype=f), (P, 1)),
                             as_cols(feature_rank),
                             path_of.reshape(NJ, P, E).transpose(1, 0, 2).reshape(P, NJ * E)], 1)

    arrays = {
        "x": a["attn_x"],
        "wqkv_t": a["attn_Wqkv_w"].T,
        "wq": a["attn_Wqkv_w"][:D],
        "out_wt": a["attn_out_w"].T,
        "w1": np.concatenate([a["ffn_W1"].transpose(1, 0, 2).reshape(D, E * DM), a["ffn_Wo1"]], 1),
        "w2": a["ffn_W2"].reshape(E * DM, D),
        "wo2": a["ffn_Wo2"],
        "b2": a["ffn_b2"],
        "cols": cols,
        "rows": rows,
        "gamma": np.tile(a["ffn_gamma"], (P, 1)),
        "beta": np.tile(a["ffn_beta"], (P, 1)),
        "out_b": np.tile(a["attn_out_b"], (P, 1)),
        "bo2": np.tile(a["ffn_bo2"], (P, 1)),
        "consts": consts,
    }
    nc = bacc.Bacc("TRN2", target_bir_lowering=False, num_devices=1)
    given, args = {}, []
    for name, v in arrays.items():
        given[name] = np.ascontiguousarray(v)
        args.append(nc.dram_tensor(name, v.shape, mybir.dt.from_np(v.dtype), kind="ExternalInput").ap())
    out = nc.dram_tensor("out", a["attn_x"].shape, F32, kind="ExternalOutput").ap()
    block_kernel(nc, *args, out)
    r = run_bass_kernel_spmd(nc, [given], core_ids=[0])
    return r.results[0]["out"]
```

```python
from contextlib import ExitStack

import concourse.bass as bass
from concourse import mybir

ALU = mybir.AluOpType
ACT = mybir.ActivationFunctionType
F32 = mybir.dt.float32
F32R = mybir.dt.float32r
BF16 = mybir.dt.bfloat16
AX_X = mybir.AxisListType.X
EPS = 1e-5

P = 128
GROUP = 4
GROUPS = 2
PAIRS = 4
GT = GROUP * P
SLOTS = 3


def block_kernel(nc, x, wqkv_t, wq, out_wt, w1, w2, wo2, b2, cols, rows, gamma, beta, out_b, bo2, consts, out):
    B, S, D = x.shape
    E = b2.shape[0]
    DM = wo2.shape[0]
    DC = D // P
    NJ = (E + 1) * DM // P
    LAST = NJ - 1
    RK = DM + E
    RL = DM + 32
    DC2 = 2 * D
    RS = 65
    assert (P, GT * GROUPS, DC, NJ, 2 * DM) == (128, S, 2, 5, P) and B % 2 == 0

    x_dram = x.rearrange("b (p t i) d -> b p i t d", i=P, t=2)
    out_dram = out.rearrange("b (p t i) d -> b p i t d", i=P, t=2)

    ctx = ExitStack()
    with ctx:
        def sb(name, shape, dt=F32):
            return ctx.enter_context(nc.sbuf_tensor(name, shape, dt))

        def sem(name):
            return ctx.enter_context(nc.semaphore(name))

        wqkvT_sb = sb("wqkvT_sb", [P, DC, 3 * D])
        wq_sb = sb("wq_sb", [P, DC, D])
        outwT_sb = sb("outwT_sb", [P, DC, D])
        w1_hi = sb("w1_hi", [P, DC, NJ * P], F32R)
        w1_lo = sb("w1_lo", [P, DC, NJ * P], F32R)
        w2_hi = sb("w2_hi", [P, NJ, D], F32R)
        w2_lo = sb("w2_lo", [P, LAST, D], F32R)
        w2_last = sb("w2_last", [P, D], F32R)
        wo2_sb = sb("wo2_sb", [P, E])
        b1_blocks = sb("b1_blocks", [P, NJ, E])
        cols_sb = sb("cols_sb", [P, cols.shape[1]])
        rows_sb = sb("rows_sb", [RS, rows.shape[1]])
        gamma_sb = sb("gamma_sb", [P, D])
        bo2_sb = sb("bo2_sb", [P, E])
        consts_sb = sb("consts_sb", [P, consts.shape[1]])
        ident_bf = sb("ident_bf", [P, P], BF16)
        bk_parts = sb("bk_parts", [RS, D], F32R)
        row_bias = sb("row_bias", [P, D])
        ident = consts_sb[:, 0:P]
        head_mask = consts_sb[:, P:2 * P]
        head_mean = consts_sb[:, 2 * P:3 * P]
        ones_col = consts_sb[:, 3 * P:3 * P + 1]
        minus_half = consts_sb[:, 3 * P + 1:3 * P + 2]
        rank = consts_sb[:, 3 * P + 2:3 * P + 2 + E]
        part_rows = consts_sb[:, 3 * P + 2 + E + NJ:3 * P + 3 + E + NJ]
        feature_rank = consts_sb[:, 3 * P + 2 + E:3 * P + 2 + E + NJ]
        path_of = consts_sb[:, 3 * P + 3 + E + NJ:].rearrange("p (j e) -> p j e", e=E)
        bq_col, gnw_col, gnb_col = cols_sb[:, 0:2], cols_sb[:, 2:4], cols_sb[:, 4:6]
        tap_col = cols_sb[:, 6:12].rearrange("p (j c) -> p j c", c=DC)
        b1_col, bo1_col = cols_sb[:, 12:12 + NJ], cols_sb[:, 12 + NJ:13 + NJ]
        bk_row, bv_row = rows_sb[:, 0:D], rows_sb[:, D:2 * D]

        x_sb = [sb(f"x_sb{q}", [P, 2 * PAIRS, D]) for q in range(2)]
        xn = [sb(f"xn{q}", [P, 2 * PAIRS, D]) for q in range(2)]
        xn_hi = sb("xn_hi", [P, GROUP, D], F32R)
        xn_half = sb("xn_half", [P, GROUP, D], F32R)
        xn_lo = sb("xn_lo", [P, GROUP, D], F32R)
        xnT = sb("xnT", [P, DC, S + 2])
        xnT_hi = sb("xnT_hi", [P, DC, S], F32R)
        xnT_lo = sb("xnT_lo", [P, DC, S], F32R)
        credits = sb("credits", [P, 7])
        col_sum = [sb(f"col_sum{q}", [P, DC, GROUPS]) for q in range(2)]
        x_stats = sb("x_stats", [P, GROUPS, GROUP, 6])
        x_mv = sb("x_mv", [P, GROUPS, GROUP, 2])
        x_var = sb("x_var", [P, GROUPS, GROUP])
        x_rstd = sb("x_rstd", [P, GROUPS, GROUP])
        x_shift = sb("x_shift", [P, GROUPS, GROUP])
        xm = sb("xm", [P, GROUPS, DC, GT])
        xm_hi = sb("xm_hi", [P, GROUPS, DC, GT], F32R)
        xm_lo = sb("xm_lo", [P, GROUPS, DC, GT], F32R)
        router_h = sb("router_h", [P, GT])
        hm = sb("hm", [P, SLOTS, GT])
        hm_hi = [sb(f"hm_hi{g}", [P, NJ, GT], F32R) for g in range(GROUPS)]
        hm_lo = [sb(f"hm_lo{g}", [P, NJ, GT], F32R) for g in range(GROUPS)]
        score = sb("score", [P, GROUP, E])
        best = sb("best", [P, GROUP])
        tied = sb("tied", [P, GROUP, E])
        chosen = sb("chosen", [P, GT], BF16)
        choice = sb("choice", [P, GROUP], BF16)
        z = sb("z", [P, 2, 2, D])
        z_stats = sb("z_stats", [P, PAIRS, 2, 6])
        z_mv = sb("z_mv", [P, PAIRS, 2, 2])
        z_var = sb("z_var", [P, PAIRS, 2])
        z_rstd = sb("z_rstd", [P, PAIRS, 2])
        out_sb = sb("out_sb", [P, 2, 2, D])
        b2_sb = out_sb[:, 0, 0, :]
        path_bias = out_sb[:, 0, 1, :]
        outb_sb = out_sb[:, 1, 0, :]
        tok_sum = sb("tok_sum", [P, DC])
        sum_all = sb("sum_all", [P, D])
        sum_rows = sb("sum_rows", [RS, 2, D], F32R)
        v_parts = sb("v_parts", [RS, D], F32R)
        mean_part = sb("mean_part", [P, DC])
        v_row = sb("v_row", [RS, D])
        gram = sb("gram", [P, DC, D])
        gram_v = sb("gram_v", [P, DC, D])
        kv = sb("kv", [P, DC, P])
        mapT = sb("mapT", [P, DC, D])
        map_ = sb("map_", [P, DC, D])
        quad = gram_v
        stat = sb("stat", [P, 6])
        head_avg = sb("head_avg", [P, DC])
        dev = sb("dev", [P, DC])
        second = sb("second", [P, DC])
        head_var = sb("head_var", [P, DC])
        head_rstd = sb("head_rstd", [P, DC])
        gn_scale = sb("gn_scale", [P, DC])
        gn_shift = sb("gn_shift", [P, DC])
        outw_scaled = map_
        attn_hi = sb("attn_hi", [P, DC, D], F32R)
        attn_lo = sb("attn_lo", [P, DC, D], F32R)
        attn_row = sb("attn_row", [P, D])

        ps_t, ps_gram, ps_chain, ps_h0, ps_h1, ps_mask, ps_ffn, ps_attn = [
            ctx.enter_context(nc.psum_tensor(n, [P, 512], F32))
            for n in ("ps_t", "ps_gram", "ps_chain", "ps_h0", "ps_h1", "ps_mask", "ps_ffn", "ps_attn")]
        ps_h = [ps_h0, ps_h1]
        w1_stage = h_flat(x_sb[1])[:, 0:DC * NJ * P]
        w2_stage = h_flat(hm)[:, 0:NJ * D]

        consts_in = sem("consts_in")
        small_in = sem("small_in")
        weights_in = sem("weights_in")
        w1_in, w2_in = sem("w1_in"), sem("w2_in")
        x_in = [[sem(f"x_in{q}{g}") for g in range(GROUPS)] for q in range(2)]
        b1_made = sem("b1_made")
        prep = sem("prep")
        bias_prod = sem("bias_prod")
        w1_hi_made, w2_hi_made = sem("w1_hi_made"), sem("w2_hi_made")
        w1_split = sem("w1_split")
        stats_chain = sem("stats_chain")
        var_ready = sem("var_ready")
        rstd_ready = sem("rstd_ready")
        shift_ready = sem("shift_ready")
        xn_ready = sem("xn_ready")
        t_ready = sem("t_ready")
        xnT_ready = sem("xnT_ready")
        xn_hi_ready = sem("xn_hi_ready")
        xn_lo_ready = sem("xn_lo_ready")
        xn_half_ready = sem("xn_half_ready")
        gram_used = sem("gram_used")
        gram_done = sem("gram_done")
        gram_read = sem("gram_read")
        center_ready = sem("center_ready")
        left_done = sem("left_done")
        xm_ready = sem("xm_ready")
        xm_hi_ready = sem("xm_hi_ready")
        xm_lo_ready = sem("xm_lo_ready")
        h_ready = sem("h_ready")
        router_hidden = sem("router_hidden")
        scores_ready = sem("scores_ready")
        router_chain = sem("router_chain")
        choice_ready = sem("choice_ready")
        route_ready = sem("route_ready")
        masked = sem("masked")
        chosen_ready = sem("chosen_ready")
        hm_hi_ready = sem("hm_hi_ready")
        hm_lo_ready = sem("hm_lo_ready")
        ffn_ready = sem("ffn_ready")
        z_done = sem("z_done")
        z_chain = sem("z_chain")
        z_var_ready = sem("z_var_ready")
        z_rstd_ready = sem("z_rstd_ready")
        xnT_hi_ready = sem("xnT_hi_ready")
        xnT_lo_ready = sem("xnT_lo_ready")
        attn_hi_ready = sem("attn_hi_ready")
        attn_ready = sem("attn_ready")
        u_done = sem("u_done")
        out_ready = sem("out_ready")
        stored = [sem(f"stored{s}") for s in range(2)]
        sum_copied = sem("sum_copied")
        tok_sum_ready = sem("tok_sum_ready")
        chain_pe = sem("chain_pe")
        chain_read = sem("chain_read")
        small_chain = sem("small_chain")
        head_var_ready = sem("head_var_ready")
        head_rstd_ready = sem("head_rstd_ready")
        scaled_ready = sem("scaled_ready")
        x_biased = sem("x_biased")

        ORDER = [LAST] + list(range(LAST))
        NSTAGE = 13
        SMALL_DMAS, WEIGHT_DMAS = 8, 3
        CREDIT = 1

        def batches(eng, first, step, tail):
            first(0, 0, 0)
            step(0, 0, (1, 0), None)
            with eng.Fori(0, B // 2 - 1) as i:
                step(i * 2 + 1, 1, (i * 2 + 2, i + 1), i * 2)
                step(i * 2 + 2, 0, (i * 2 + 3, i + 1), i * 2 + 1)
            step(B - 1, 1, None, B - 2)
            tail(B - 1, 1)

        block = ctx.enter_context(nc.Block())

        @block.sync
        def _(sp):
            def load(nb, q, g):
                for p in (2 * g, 2 * g + 1):
                    sp.dma_start(x_sb[q][:, 2 * p:2 * p + 2, :], x_dram[nb, p]).then_inc(x_in[q][g], 16)

            load(0, 0, 0)
            sp.dma_start(consts_sb[:, :], consts).then_inc(consts_in, 16)
            load(0, 0, 1)
            sp.dma_start(cols_sb[:, :], cols).then_inc(consts_in, 16)
            sp.dma_start(w1_stage.rearrange("p (c n) -> p c n", c=DC),
                         w1.rearrange("(c p) n -> p c n", p=P)).then_inc(w1_in, 16)
            sp.dma_start(w2_stage[:, 0:LAST * D].rearrange("p (j n) -> p j n", n=D),
                         w2[0:LAST * P, :].rearrange("(j p) n -> p j n", p=P)).then_inc(w2_in, 16)
            for r in (0, DM):
                sp.dma_start(w2_stage[r:r + DM, LAST * D:NJ * D], w2[LAST * P:E * DM, :]).then_inc(w2_in, 16)
            sp.dma_start(rows_sb[:, :], rows).then_inc(small_in, 16)
            for r in (DM, RL):
                sp.dma_start(b2_sb[r:r + E, :], b2).then_inc(small_in, 16)
            sp.dma_start(wo2_sb[DM:P, :], wo2).then_inc(small_in, 16)
            sp.dma_start(bo2_sb[:, :], bo2).then_inc(small_in, 16)
            sp.dma_start(wqkvT_sb[:, :, :], wqkv_t.rearrange("(c p) n -> p c n", p=P)).then_inc(weights_in, 16)
            sp.dma_start(row_bias[:, :], beta).then_inc(small_in, 16)
            sp.dma_start(outb_sb[:, :], out_b).then_inc(small_in, 16)
            sp.dma_start(gamma_sb[:, :], gamma).then_inc(small_in, 16)
            sp.dma_start(wq_sb[:, :, :], wq.rearrange("(c p) n -> p c n", p=P)).then_inc(weights_in, 16)
            sp.dma_start(outwT_sb[:, :, :], out_wt.rearrange("(c p) n -> p c n", p=P)).then_inc(weights_in, 16)

            def store(b, p):
                sp.wait_ge(out_ready, CREDIT + PAIRS * b + p + 1)
                sp.dma_start(out_dram[b, p], out_sb[:, p % 2, :, :]).then_inc(stored[p % 2], 16)

            def first(nb, half, q):
                pass

            def step(b, q, nxt, prev):
                if nxt:
                    if prev is not None:
                        sp.wait_ge(out_ready, CREDIT + PAIRS * prev + 2)
                    else:
                        sp.wait_ge(w1_split, 1)
                    load(nxt[0], 1 - q, 0)
                if prev is not None:
                    store(prev, 2)
                    store(prev, 3)
                if nxt:
                    load(nxt[0], 1 - q, 1)
                store(b, 0)
                store(b, 1)

            def tail(b, q):
                store(b, 2)
                store(b, 3)

            batches(sp, first, step, tail)
            for s in range(2):
                sp.wait_ge(stored[s], 16 * (CREDIT + 2 * B))

        @block.gpsimd
        def _(pool):
            pool.wait_ge(consts_in, 32)

            def w1_low():
                pool.wait_ge(w1_hi_made, 1)
                nc.gpsimd.tensor_tensor(w1_lo[:, :, :], w1_stage.rearrange("p (c n) -> p c n", c=DC),
                                        w1_hi[:, :, :].bitcast(F32), ALU.subtract).then_inc(w1_split, 1)

            def x_pow(nb, g):
                pool.wait_ge(var_ready, 2 * nb + g + 1)
                nc.gpsimd.tensor_tensor(x_rstd[:, g, :], x_var[:, g, :],
                                        minus_half.to_broadcast([P, GROUP]), ALU.pow).then_inc(rstd_ready, 1)

            def normalise(nb, q, g):
                pool.wait_ge(shift_ready, 2 * nb + g + 1)
                pool.nop(nofuse=True)
                for t in range(GROUP):
                    nc.gpsimd.tensor_scalar(xn[q][:, GROUP * g + t, :], x_sb[q][:, GROUP * g + t, :],
                                            x_rstd[:, g, t:t + 1], x_shift[:, g, t:t + 1],
                                            ALU.mult, ALU.add).then_inc(xn_ready, 1)

            def mixed_low(b, g):
                for c in range(DC):
                    pool.wait_ge(xm_hi_ready, 4 * b + 2 * g + c + 1)
                    nc.gpsimd.tensor_tensor(xm_lo[:, g, c, :], xm[:, g, c, :], xm_hi[:, g, c, :].bitcast(F32),
                                            ALU.subtract).then_inc(xm_lo_ready, 1)

            def hidden_low(b, g, k):
                j = ORDER[k]
                r = DM if j == LAST else P
                pool.wait_ge(hm_hi_ready, 10 * b + NJ * g + k + 1)
                nc.gpsimd.tensor_tensor(hm_lo[g][0:r, j, :], hm[0:r, k % SLOTS, :], hm_hi[g][0:r, j, :].bitcast(F32),
                                        ALU.subtract).then_inc(hm_lo_ready, 1)

            def z_pow(b, p):
                pool.wait_ge(z_var_ready, 4 * b + p + 1)
                nc.gpsimd.tensor_tensor(z_rstd[:, p, :], z_var[:, p, :], minus_half.to_broadcast([P, 2]),
                                        ALU.pow).then_inc(z_rstd_ready, 1)

            def bias_x(b, q, p):
                pool.wait_ge(chain_read, CREDIT + NSTAGE * (b + 1))
                nc.gpsimd.tensor_tensor(x_sb[q][:, 2 * p:2 * p + 2, :], x_sb[q][:, 2 * p:2 * p + 2, :],
                                        attn_row[:, :].rearrange("p (o n) -> p o n", o=1).to_broadcast([P, 2, D]),
                                        ALU.add).then_inc(x_biased, 1)

            def final(b, q, p):
                pool.wait_ge(x_biased, 4 * b + p + 1)
                pool.wait_ge(u_done, CREDIT + 4 * b + p + 1)
                nc.gpsimd.tensor_tensor(out_sb[:, p % 2, :, :], out_sb[:, p % 2, :, :],
                                        x_sb[q][:, 2 * p:2 * p + 2, :], ALU.add).then_inc(out_ready, 1)

            def head_pow(b):
                pool.wait_ge(head_var_ready, b + 1)
                nc.gpsimd.tensor_tensor(head_rstd[:, :], head_var[:, :], minus_half.to_broadcast([P, DC]),
                                        ALU.pow).then_inc(head_rstd_ready, 1)

            def first(nb, half, q):
                for g in range(GROUPS):
                    x_pow(nb, g)
                    normalise(nb, q, g)
                w1_low()
                mixed_low(nb, 0)

            def step(b, q, nxt, prev):
                if prev is not None:
                    z_pow(prev, 2)
                    bias_x(prev, 1 - q, 2)
                    bias_x(prev, 1 - q, 3)
                if nxt:
                    x_pow(nxt[0], 0)
                    normalise(nxt[0], 1 - q, 0)
                hidden_low(b, 0, 0)
                if prev is not None:
                    final(prev, 1 - q, 2)
                mixed_low(b, 1)
                if prev is not None:
                    z_pow(prev, 3)
                hidden_low(b, 0, 1)
                if prev is not None:
                    final(prev, 1 - q, 3)
                hidden_low(b, 0, 2)
                hidden_low(b, 0, 3)
                hidden_low(b, 0, 4)
                if nxt:
                    x_pow(nxt[0], 1)
                head_pow(b)
                if nxt:
                    normalise(nxt[0], 1 - q, 1)
                hidden_low(b, 1, 0)
                hidden_low(b, 1, 1)
                hidden_low(b, 1, 2)
                z_pow(b, 0)
                hidden_low(b, 1, 3)
                hidden_low(b, 1, 4)
                if nxt:
                    mixed_low(nxt[0], 0)
                bias_x(b, q, 0)
                z_pow(b, 1)
                final(b, q, 0)
                bias_x(b, q, 1)
                final(b, q, 1)

            def tail(b, q):
                z_pow(b, 2)
                for p in (2, 3):
                    bias_x(b, q, p)
                final(b, q, 2)
                z_pow(b, 3)
                final(b, q, 3)

            batches(pool, first, step, tail)

        @block.scalar
        def _(act):
            def w1_high():
                act.wait_ge(w1_in, 16)
                nc.scalar.activation(w1_hi[:, :, :], w1_stage.rearrange("p (c n) -> p c n", c=DC),
                                     ACT.Copy).then_inc(w1_hi_made, 1)

            def w2_high():
                act.wait_ge(w2_in, 48)
                nc.scalar.activation(w2_hi[:, 0:LAST, :], w2_stage[:, 0:LAST * D].rearrange("p (j n) -> p j n", n=D),
                                     ACT.Copy)
                nc.scalar.activation(w2_hi[0:DM, LAST, :], w2_stage[0:DM, LAST * D:NJ * D], ACT.Copy)
                nc.scalar.activation(w2_last[:, :], w2_stage[:, LAST * D:NJ * D], ACT.Copy).then_inc(w2_hi_made, 1)

            def xn_high(nb, q, g, half):
                if half == 0 and not (isinstance(nb, int) and nb == 0 and g == 0):
                    act.wait_ge(gram_used, 2 * nb + g)
                act.wait_ge(xn_ready, 8 * nb + GROUP * g + 2 * half + 2)
                tiles, own = slice(2 * half, 2 * half + 2), slice(GROUP * g + 2 * half, GROUP * g + 2 * half + 2)
                nc.scalar.activation(xn_hi[:, tiles, :], xn[q][:, own, :], ACT.Copy).then_inc(xn_hi_ready, 1)
                nc.scalar.activation(xn_half[:, tiles, :], xn[q][:, own, :], ACT.Copy,
                                     scale=0.5).then_inc(xn_half_ready, 1)

            def transposed(nb, q, g, c):
                if c == 0 and not (isinstance(nb, int) and nb == 0):
                    act.wait_ge(xm_ready, 4 * nb)
                    act.wait_ge(xnT_lo_ready, 2 * nb + g - 1)
                act.wait_ge(t_ready, 4 * nb + 2 * g + c + 1)
                nc.scalar.activation(xnT[:, c, 1 + GT * g:1 + GT * (g + 1)], ps_t[:, :], ACT.Copy,
                                     accum_out=col_sum[q][:, c, g:g + 1]).then_inc(xnT_ready, 1)

            def attention_high(b, g):
                if not (isinstance(b, int) and b == 0):
                    act.wait_ge(attn_ready, 4 * b + 2 * g - 2)
                act.wait_ge(xnT_ready, 4 * b + 4)
                nc.scalar.activation(xnT_hi[:, :, GT * g:GT * (g + 1)], xnT[:, :, 1 + GT * g:1 + GT * (g + 1)],
                                     ACT.Copy).then_inc(xnT_hi_ready, 1)

            def center(b, q, g):
                act.wait_ge(xnT_ready, 4 * b + 2 * g + 2)
                for c in range(DC):
                    nc.scalar.activation(xm[:, g, c, :], xnT[:, c, 1 + GT * g:1 + GT * (g + 1)], ACT.Copy,
                                         scale=tap_col[:, 1, c:c + 1]).then_inc(center_ready, 1)

            def mixed_high(b, g):
                for c in range(DC):
                    act.wait_ge(xm_ready, 4 * b + 2 * g + c + 1)
                    nc.scalar.activation(xm_hi[:, g, c, :], xm[:, g, c, :], ACT.Copy).then_inc(xm_hi_ready, 1)

            def router(b, g):
                act.wait_ge(h_ready, 10 * b + NJ * g + 1)
                nc.scalar.activation(router_h[DM:P, :], ps_h[(NJ * g) % 2][DM:P, :], ACT.Tanh,
                                     bias=bo1_col[DM:P, :]).then_inc(router_hidden, 1)

            def choices(b, g):
                act.wait_ge(route_ready, 2 * b + g + 1)
                nc.scalar.activation(chosen[:, :], ps_mask[:, :], ACT.Copy).then_inc(chosen_ready, 1)

            def hidden_high(b, g, k):
                j = ORDER[k]
                r = DM if j == LAST else P
                act.wait_ge(masked, CREDIT + 10 * b + NJ * g + k + 1)
                if j == LAST:
                    nc.scalar.activation(hm_lo[g][DM:P, j, :], hm[0:DM, k % SLOTS, :], ACT.Copy)
                nc.scalar.activation(hm_hi[g][0:r, j, :], hm[0:r, k % SLOTS, :], ACT.Copy).then_inc(hm_hi_ready, 1)

            def read_stage(b, s, dst):
                act.wait_ge(chain_pe, NSTAGE * b + s + 1)
                nc.scalar.activation(dst, ps_chain[:, :].rearrange("p (c n) -> p c n", c=DC),
                                     ACT.Copy).then_inc(chain_read, 1)

            def copy_sum(b):
                act.wait_ge(chain_pe, NSTAGE * b + 1)
                nc.scalar.activation(sum_all[:, :], ps_chain[:, 0:D], ACT.Copy).then_inc(sum_copied, 1)

            def read_attention(b):
                act.wait_ge(chain_pe, NSTAGE * b + 12)
                nc.scalar.activation(attn_hi[:, :, :], ps_chain[:, :].rearrange("p (c n) -> p c n", c=DC),
                                     ACT.Copy).then_inc(attn_hi_ready, 1)

            def read_gram(b):
                act.wait_ge(gram_done, b + 1)
                nc.scalar.activation(gram[:, :, :], ps_gram[:, :].rearrange("p (c n) -> p c n", c=DC),
                                     ACT.Copy).then_inc(gram_read, 1)

            def first(nb, half, q):
                act.wait_ge(consts_in, 32)
                xn_high(nb, q, 0, 0)
                transposed(nb, q, 0, 0)
                w1_high()
                transposed(nb, q, 0, 1)
                xn_high(nb, q, 0, 1)
                transposed(nb, q, 1, 0)
                center(nb, q, 0)
                transposed(nb, q, 1, 1)
                for h in range(2):
                    xn_high(nb, q, 1, h)
                mixed_high(nb, 0)
                w2_high()

            def step(b, q, nxt, prev):
                attention_high(b, 0)
                copy_sum(b)
                router(b, 0)
                read_gram(b)
                center(b, q, 1)
                choices(b, 0)
                read_stage(b, 3, gram_v[:, :, :])
                hidden_high(b, 0, 0)
                mixed_high(b, 1)
                hidden_high(b, 0, 1)
                hidden_high(b, 0, 2)
                read_stage(b, 5, mapT[:, :, :])
                if nxt:
                    xn_high(nxt[0], 1 - q, 0, 0)
                hidden_high(b, 0, 3)
                read_stage(b, 6, map_[:, :, :])
                if nxt:
                    xn_high(nxt[0], 1 - q, 0, 1)
                router(b, 1)
                if nxt:
                    transposed(nxt[0], 1 - q, 0, 0)
                hidden_high(b, 0, 4)
                attention_high(b, 1)
                choices(b, 1)
                hidden_high(b, 1, 0)
                if nxt:
                    transposed(nxt[0], 1 - q, 0, 1)
                    xn_high(nxt[0], 1 - q, 1, 0)
                    transposed(nxt[0], 1 - q, 1, 0)
                hidden_high(b, 1, 1)
                hidden_high(b, 1, 2)
                read_attention(b)
                if nxt:
                    transposed(nxt[0], 1 - q, 1, 1)
                    center(nxt[0], 1 - q, 0)
                hidden_high(b, 1, 3)
                hidden_high(b, 1, 4)
                if nxt:
                    xn_high(nxt[0], 1 - q, 1, 1)
                    mixed_high(nxt[0], 0)

            def tail(b, q):
                pass

            batches(act, first, step, tail)

        @block.vector
        def _(dve):
            def link(ins, s, value):
                ins.then_inc(s, 1)
                dve.wait_ge(s, value)

            for at in (0, S + 1):
                nc.vector.memset(xnT[:, :, at:at + 1], 0.0)
            nc.vector.memset(w2_hi[DM:P, LAST, :].bitcast(F32), 0.0)
            free = [(masked, 1), (z_done, 1), (u_done, 1), (chain_read, 1), (out_ready, 1),
                    (stored[0], 16), (stored[1], 16)]
            for i, (s, credit) in enumerate(free):
                nc.vector.memset(credits[:, i:i + 1], 0.0).then_inc(s, credit)

            def constants():
                dve.wait_ge(small_in, 16 * SMALL_DMAS)
                nc.vector.tensor_copy(ident_bf[:, :], ident)
                link(nc.vector.tensor_scalar(bk_parts[:, :], bk_row, part_rows[0:RS, :], float(S), ALU.mult, ALU.mult),
                     prep, 1)
                nc.vector.scalar_tensor_tensor(bk_parts[64:65, :], bk_row[64:65, :], float(S),
                                               bk_parts[64:65, :].bitcast(F32), ALU.mult, ALU.subtract)
                nc.vector.tensor_tensor(row_bias[:, :], row_bias[:, :], outb_sb[:, :], ALU.add).then_inc(prep, 1)

            def bias_blocks():
                dve.wait_ge(consts_in, 32)
                nc.vector.tensor_tensor(b1_blocks[:, :, :], path_of,
                                        b1_col.rearrange("p (j a) -> p j a", a=1).to_broadcast([P, NJ, E]),
                                        ALU.mult).then_inc(b1_made, 1)

            def w2_low():
                dve.wait_ge(w2_hi_made, 1)
                nc.vector.tensor_tensor(w2_lo[:, :, :], w2_stage[:, 0:LAST * D].rearrange("p (j n) -> p j n", n=D),
                                        w2_hi[:, 0:LAST, :].bitcast(F32), ALU.subtract)
                nc.vector.tensor_tensor(w2_last[DM:P, :], w2_stage[DM:P, LAST * D:NJ * D],
                                        w2_last[DM:P, :].bitcast(F32), ALU.subtract).then_inc(prep, 1)

            def path_biases():
                dve.wait_ge(bias_prod, 1)
                hi, lo = slice(DM, RK), slice(RL, RL + E)
                for r in (hi, lo):
                    last = nc.vector.tensor_tensor(path_bias[r, :], ps_ffn[r, 0:D], b2_sb[r, :], ALU.add)
                link(last, prep, 4)
                for r in (hi, lo):
                    last = nc.vector.tensor_copy(w2_hi[r, LAST, :], path_bias[r, :])
                link(last, prep, 5)
                nc.vector.tensor_tensor(w2_hi[lo, LAST, :], path_bias[lo, :], w2_hi[lo, LAST, :].bitcast(F32),
                                        ALU.subtract).then_inc(prep, 1)

            def x_statistics(nb, half, q, g):
                dve.wait_ge(x_in[q][g], 32 * (half + 1))
                for t in range(GROUP):
                    last = nc.vector.bn_stats(x_stats[:, g, t, :], x_sb[q][:, GROUP * g + t, :])
                link(last, stats_chain, 4 * nb + 2 * g + 1)
                dve.nop(nofuse=True)
                for t in range(GROUP):
                    last = nc.vector.bn_aggr(x_mv[:, g, t, :], x_stats[:, g, t, :])
                link(last, stats_chain, 4 * nb + 2 * g + 2)
                nc.vector.tensor_scalar(x_var[:, g, :], x_mv[:, g, :, 1], EPS, None, ALU.add).then_inc(var_ready, 1)

            def xn_low(nb, q, g, half):
                dve.wait_ge(xn_hi_ready, 4 * nb + 2 * g + half + 1)
                tiles, own = slice(2 * half, 2 * half + 2), slice(GROUP * g + 2 * half, GROUP * g + 2 * half + 2)
                nc.vector.tensor_tensor(xn_lo[:, tiles, :], xn[q][:, own, :], xn_hi[:, tiles, :].bitcast(F32),
                                        ALU.subtract).then_inc(xn_lo_ready, 1)

            def x_offset(nb, g):
                dve.wait_ge(rstd_ready, 2 * nb + g + 1)
                nc.vector.scalar_tensor_tensor(x_shift[:, g, :], x_mv[:, g, :, 0], -1.0, x_rstd[:, g, :],
                                               ALU.mult, ALU.mult).then_inc(shift_ready, 1)

            def mix(b, q, g):
                dve.wait_ge(xnT_ready, 4 * b + 4)
                for c in range(DC):
                    n = 4 * b + 2 * g + c + 1
                    dve.wait_ge(center_ready, n)
                    link(nc.vector.scalar_tensor_tensor(xm[:, g, c, :], xnT[:, c, GT * g:GT * (g + 1)],
                                                        tap_col[:, 0, c:c + 1], xm[:, g, c, :],
                                                        ALU.mult, ALU.add), left_done, n)
                    nc.vector.scalar_tensor_tensor(xm[:, g, c, :], xnT[:, c, 2 + GT * g:2 + GT * (g + 1)],
                                                   tap_col[:, 2, c:c + 1], xm[:, g, c, :],
                                                   ALU.mult, ALU.add).then_inc(xm_ready, 1)

            def choose(b, g):
                n = 8 * b + 4 * g
                dve.wait_ge(scores_ready, 2 * b + g + 1)

                link(nc.vector.tensor_tensor(score[:, :, :], ps_mask[:, 0:GROUP * E].rearrange("p (t e) -> p t e", e=E),
                                             bo2_sb[:, :].rearrange("p (o e) -> p o e", o=1).to_broadcast([P, GROUP, E]),
                                             ALU.add), router_chain, n + 1)
                link(nc.vector.tensor_reduce(best[:, :], score[:, :, :], AX_X, ALU.max), router_chain, n + 2)
                link(nc.vector.tensor_tensor(tied[:, :, :], score[:, :, :],
                                             best[:, :].rearrange("p (t o) -> p t o", o=1).to_broadcast([P, GROUP, E]),
                                             ALU.is_equal), router_chain, n + 3)
                link(nc.vector.tensor_tensor(tied[:, :, :], tied[:, :, :],
                                             rank.rearrange("p (o e) -> p o e", o=1).to_broadcast([P, GROUP, E]),
                                             ALU.mult), router_chain, n + 4)
                nc.vector.tensor_reduce(choice[:, :], tied[:, :, :], AX_X, ALU.max).then_inc(choice_ready, 1)

            def path_rows(b, g):
                dve.wait_ge(chosen_ready, 2 * b + g + 1)
                nc.vector.tensor_scalar(hm_hi[g][DM:P, LAST, :], chosen[DM:P, :], feature_rank[DM:P, LAST:NJ],
                                        None, ALU.is_equal)

            def mask(b, g, k):
                n = 10 * b + NJ * g + k + 1
                j = ORDER[k]
                r = DM if j == LAST else P
                dve.wait_ge(h_ready, n)
                before = NJ - SLOTS if k < NJ - SLOTS else SLOTS
                if not (isinstance(n, int) and n <= SLOTS):
                    dve.wait_ge(hm_lo_ready, n - before)
                nc.vector.scalar_tensor_tensor(hm[0:r, k % SLOTS, :], chosen[0:r, :], feature_rank[0:r, j:j + 1],
                                               ps_h[(NJ * g + k) % 2][0:r, :], ALU.is_equal,
                                               ALU.mult).then_inc(masked, 1)

            def z_statistics(b, q, p):
                n = 4 * b + p + 1
                dve.wait_ge(ffn_ready, n)
                link(nc.vector.tensor_tensor(z[:, p % 2, :, :], ps_ffn[:, :].rearrange("p (t n) -> p t n", t=2),
                                             xn[q][:, 2 * p:2 * p + 2, :], ALU.add), z_done, CREDIT + n)
                for t in range(2):
                    last = nc.vector.bn_stats(z_stats[:, p, t, :], z[:, p % 2, t, :])
                link(last, z_chain, 3 * n - 2)
                dve.nop(nofuse=True)
                for t in range(2):
                    last = nc.vector.bn_aggr(z_mv[:, p, t, :], z_stats[:, p, t, :])
                link(last, z_chain, 3 * n - 1)
                nc.vector.tensor_scalar(z_var[:, p, :], z_mv[:, p, :, 1], EPS, None, ALU.add).then_inc(z_var_ready, 1)
                for t in range(2):
                    last = nc.vector.scalar_tensor_tensor(z[:, p % 2, t, :], z[:, p % 2, t, :], z_mv[:, p, t, 0:1],
                                                          gamma_sb[:, :], ALU.subtract, ALU.mult)
                link(last, z_chain, 3 * n)

            def combine(b, p):
                n = 4 * b + p + 1
                dve.wait_ge(z_rstd_ready, n)
                dve.wait_ge(attn_ready, n)
                dve.wait_ge(stored[p % 2], 16 * CREDIT + 16 * (2 * b + p // 2))
                for t in range(2):
                    last = nc.vector.scalar_tensor_tensor(out_sb[:, p % 2, t, :], z[:, p % 2, t, :], z_rstd[:, p, t:t + 1],
                                                          ps_attn[:, D * t:D * (t + 1)], ALU.mult, ALU.add)
                last.then_inc(u_done, 1)

            def stage(b, s):
                dve.wait_ge(chain_pe, NSTAGE * b + s + 1)

            def attention_low(b, g):
                dve.wait_ge(xnT_hi_ready, 2 * b + g + 1)
                nc.vector.tensor_tensor(xnT_lo[:, :, GT * g:GT * (g + 1)], xnT[:, :, 1 + GT * g:1 + GT * (g + 1)],
                                        xnT_hi[:, :, GT * g:GT * (g + 1)].bitcast(F32),
                                        ALU.subtract).then_inc(xnT_lo_ready, 1)

            def token_sum(b, q):
                dve.wait_ge(xnT_ready, 4 * b + 4)
                nc.vector.tensor_tensor(tok_sum[:, :], col_sum[q][:, :, 0], col_sum[q][:, :, 1],
                                        ALU.add).then_inc(tok_sum_ready, 1)

            def sum_parts(b):
                dve.wait_ge(sum_copied, b + 1)
                nc.vector.tensor_scalar(sum_rows[:, 0, :], ps_chain[0:RS, 0:D], part_rows[0:RS, :], None, ALU.mult)
                link(nc.vector.tensor_scalar(sum_rows[:, 1, :], ps_chain[0:RS, 0:D], -0.5 / S, None, ALU.mult),
                     small_chain, 8 * b + 1)
                nc.vector.tensor_tensor(sum_rows[64:65, 0, :], ps_chain[64:65, 0:D], sum_rows[64:65, 0, :].bitcast(F32),
                                        ALU.subtract)
                nc.vector.scalar_tensor_tensor(sum_rows[32:33, 1, :], ps_chain[32:33, 0:D], -0.5 / S,
                                               sum_rows[32:33, 1, :].bitcast(F32), ALU.mult,
                                               ALU.subtract).then_inc(chain_read, 1)

            def mean_value(b):
                stage(b, 1)
                link(nc.vector.scalar_tensor_tensor(v_row[:, :], ps_chain[0:RS, 0:D], 1.0 / S, bv_row,
                                                    ALU.mult, ALU.add), small_chain, 8 * b + 2)
                link(nc.vector.tensor_copy(v_parts[:, :], v_row[:, :]), small_chain, 8 * b + 3)
                nc.vector.tensor_tensor(v_parts[32:33, :], v_row[32:33, :], v_parts[32:33, :].bitcast(F32),
                                        ALU.subtract).then_inc(chain_read, 1)

            def feature_means(b):
                dve.wait_ge(chain_read, CREDIT + NSTAGE * b + 6)
                for c in range(DC):
                    last = nc.vector.scalar_tensor_tensor(quad[:, c, :], mapT[:, c, :], 1.0 / S, sum_all[:, :],
                                                          ALU.mult, ALU.mult, accum_out=mean_part[:, c:c + 1])
                link(last, small_chain, 8 * b + 4)

            def symmetric(b):
                stage(b, 2)
                dve.wait_ge(gram_read, b + 1)
                nc.vector.tensor_tensor(gram[:, :, :], gram[:, :, :], ps_chain[:, :].rearrange("p (c n) -> p c n", c=DC),
                                        ALU.add).then_inc(chain_read, 1)

            def head_blocks(b):
                stage(b, 4)
                nc.vector.tensor_tensor(kv[:, :, :], ps_chain[:, 0:DC * P].rearrange("p (c n) -> p c n", c=DC),
                                        head_mask.rearrange("p (o n) -> p o n", o=1).to_broadcast([P, DC, P]),
                                        ALU.mult).then_inc(chain_read, 1)

            def quadratic(b):
                stage(b, 7)
                for c in range(DC):
                    last = nc.vector.scalar_tensor_tensor(quad[:, c, :], ps_chain[:, D * c:D * (c + 1)], 1.0,
                                                          mapT[:, c, :], ALU.mult, ALU.mult,
                                                          accum_out=stat[:, c:c + 1])
                last.then_inc(chain_read, 1)

            def feature_stats(b):
                stage(b, 8)
                nc.vector.tensor_tensor(stat[:, 2:6:2], ps_chain[:, 0:DC], mean_part[:, :], ALU.add)
                nc.vector.tensor_copy(stat[:, 3:6:2], ps_chain[:, 0:DC]).then_inc(chain_read, 1)

            def spread_in_head(b):
                stage(b, 9)
                n = 8 * b + 4
                nc.vector.tensor_copy(head_avg[:, :], ps_chain[:, 0:DC])
                link(nc.vector.tensor_tensor(dev[:, :], stat[:, 2:6:2], ps_chain[:, 0:DC], ALU.subtract),
                     small_chain, n + 1)
                link(nc.vector.tensor_tensor(dev[:, :], dev[:, :], dev[:, :], ALU.mult), small_chain, n + 2)
                nc.vector.scalar_tensor_tensor(second[:, :], stat[:, 0:DC], 1.0 / S, dev[:, :],
                                               ALU.mult, ALU.add).then_inc(chain_read, 1)

            def head_variance(b):
                stage(b, 10)
                nc.vector.tensor_scalar(head_var[:, :], ps_chain[:, 0:DC], EPS, None, ALU.add)\
                    .then_inc(head_var_ready, 1)

            def group_norm(b):
                dve.wait_ge(head_rstd_ready, b + 1)
                nc.vector.tensor_tensor(gn_shift[:, :], stat[:, 3:6:2], head_avg[:, :], ALU.subtract)
                link(nc.vector.tensor_tensor(gn_scale[:, :], head_rstd[:, :], gnw_col, ALU.mult),
                     small_chain, 8 * b + 7)
                link(nc.vector.tensor_tensor(gn_shift[:, :], gn_shift[:, :], gn_scale[:, :], ALU.mult),
                     small_chain, 8 * b + 8)
                nc.vector.tensor_tensor(gn_shift[:, :], gn_shift[:, :], gnb_col, ALU.add).then_inc(chain_read, 1)
                for c in range(DC):
                    last = nc.vector.tensor_scalar(outw_scaled[:, c, :], outwT_sb[:, c, :], gn_scale[:, c:c + 1],
                                                   None, ALU.mult)
                last.then_inc(scaled_ready, 1)

            def matrix_low(b):
                dve.wait_ge(attn_hi_ready, b + 1)
                nc.vector.tensor_tensor(attn_lo[:, :, :], ps_chain[:, :].rearrange("p (c n) -> p c n", c=DC),
                                        attn_hi[:, :, :].bitcast(F32), ALU.subtract).then_inc(chain_read, 1)

            def attention_row(b):
                stage(b, 12)
                if not isinstance(b, int) or b > 0:
                    dve.wait_ge(x_biased, PAIRS * b)
                nc.vector.tensor_tensor(attn_row[:, :], ps_chain[:, 0:D], row_bias[:, :],
                                        ALU.add).then_inc(chain_read, 1)

            def first(nb, half, q):
                for g in range(GROUPS):
                    x_statistics(nb, half, q, g)
                    x_offset(nb, g)
                xn_low(nb, q, 0, 0)
                bias_blocks()
                xn_low(nb, q, 0, 1)
                constants()
                mix(nb, q, 0)
                token_sum(nb, q)
                for h in range(2):
                    xn_low(nb, q, 1, h)
                w2_low()
                path_biases()

            def step(b, q, nxt, prev):
                sum_parts(b)
                if prev is not None:
                    z_statistics(prev, 1 - q, 2)
                mean_value(b)
                choose(b, 0)
                symmetric(b)
                if nxt:
                    x_statistics(*nxt, 1 - q, 0)
                if prev is not None:
                    combine(prev, 2)
                path_rows(b, 0)
                mask(b, 0, 0)
                mask(b, 0, 1)
                if nxt:
                    x_offset(nxt[0], 0)
                mix(b, q, 1)
                head_blocks(b)
                mask(b, 0, 2)
                if prev is not None:
                    z_statistics(prev, 1 - q, 3)
                mask(b, 0, 3)
                feature_means(b)
                if prev is not None:
                    combine(prev, 3)
                attention_low(b, 0)
                mask(b, 0, 4)
                if nxt:
                    xn_low(nxt[0], 1 - q, 0, 0)
                quadratic(b)
                choose(b, 1)
                if nxt:
                    xn_low(nxt[0], 1 - q, 0, 1)
                feature_stats(b)
                if nxt:
                    x_statistics(*nxt, 1 - q, 1)
                spread_in_head(b)
                path_rows(b, 1)
                mask(b, 1, 0)
                if nxt:
                    x_offset(nxt[0], 1)
                head_variance(b)
                mask(b, 1, 1)
                attention_low(b, 1)
                group_norm(b)
                mask(b, 1, 2)
                z_statistics(b, q, 0)
                if nxt:
                    xn_low(nxt[0], 1 - q, 1, 0)
                mask(b, 1, 3)
                matrix_low(b)
                mask(b, 1, 4)
                if nxt:
                    mix(nxt[0], 1 - q, 0)
                combine(b, 0)
                if nxt:
                    xn_low(nxt[0], 1 - q, 1, 1)
                    token_sum(nxt[0], 1 - q)
                attention_row(b)
                z_statistics(b, q, 1)
                combine(b, 1)

            def tail(b, q):
                for p in (2, 3):
                    z_statistics(b, q, p)
                    combine(b, p)

            batches(dve, first, step, tail)

        @block.tensor
        def _(pe):
            mm = nc.tensor.matmul
            def bias_products():
                pe.wait_ge(b1_made, 1)
                pe.wait_ge(w2_in, 48)
                for j in range(NJ):
                    r = DM if j == LAST else P
                    for at in (DM, RL):
                        last = mm(ps_ffn[at:at + E, 0:D], b1_blocks[0:r, j, :], w2_stage[0:r, j * D:(j + 1) * D],
                                  start=(j == 0), stop=(j == LAST), skip_group_check=True)
                last.then_inc(bias_prod, 1)

            def transposes(nb, q, g, c):
                pe.wait_ge(xnT_ready, 4 * nb + 2 * g + c)
                for t in range(GROUP):
                    if c == 0:
                        pe.wait_ge(xn_ready, 8 * nb + GROUP * g + t + 1)
                    last = nc.tensor.transpose(ps_t[:, P * t:P * (t + 1)], xn[q][:, GROUP * g + t, P * c:P * (c + 1)],
                                               ident)
                last.then_inc(t_ready, 1)

            def gram_tiles(nb, q, g, half):
                if g == 0 and half == 0:
                    pe.wait_ge(gram_read, nb)
                pe.wait_ge(xn_half_ready, 4 * nb + 2 * g + half + 1)
                pe.wait_ge(xn_lo_ready, 4 * nb + 2 * g + half + 1)
                for t in (2 * half, 2 * half + 1):
                    for c in range(DC):
                        for rhs in (xn_half, xn_lo):
                            last = mm(ps_gram[:, D * c:D * (c + 1)], xn_hi[:, t, P * c:P * (c + 1)], rhs[:, t, :],
                                      start=(g == 0 and t == 0 and c == 0 and rhs is xn_half), stop=False,
                                      skip_group_check=True)
                if half == 1:
                    last.then_inc(gram_used, 1)

            def split_mm(ps, parts, started=False, ended=True):
                todo = [(a, r) for lh, ll, rh, rl in parts for a, r in ((lh, rh), (lh, rl), (ll, rh))]
                for i, (a, r) in enumerate(todo):
                    last = mm(ps, a, r, start=(i == 0 and not started), stop=(i == len(todo) - 1 and ended))
                return last

            def hidden(b, g, k):
                j = ORDER[k]
                if k == 0:
                    pe.wait_ge(xm_hi_ready, 4 * b + 2 * g + 2)
                    pe.wait_ge(xm_lo_ready, 4 * b + 2 * g + 2)
                pe.wait_ge(masked, CREDIT + 10 * b + NJ * g + k - (1 if NJ * g + k else 0))
                cols_j = slice(P * j, P * (j + 1))
                split_mm(ps_h[(NJ * g + k) % 2][:, :],
                         [(w1_hi[:, c, cols_j], w1_lo[:, c, cols_j], xm_hi[:, g, c, :], xm_lo[:, g, c, :])
                          for c in range(DC)]).then_inc(h_ready, 1)

            def scores(b, g):
                pe.wait_ge(router_hidden, 2 * b + g + 1)
                pe.wait_ge(chosen_ready, 2 * b + g)
                for t in range(GROUP):
                    last = mm(ps_mask[:, E * t:E * (t + 1)], router_h[DM:P, P * t:P * (t + 1)], wo2_sb[DM:P, :],
                              start=True, stop=True)
                last.then_inc(scores_ready, 1)

            def route(b, g):
                pe.wait_ge(choice_ready, 2 * b + g + 1)
                for t in range(GROUP):
                    last = mm(ps_mask[:, P * t:P * (t + 1)], choice[:, t:t + 1].to_broadcast([P, P]), ident_bf[:, :],
                              start=True, stop=True)
                last.then_inc(route_ready, 1)

            def ffn(b, p, t):
                g = p // 2
                if t == 0:
                    if p % 2 == 0:
                        pe.wait_ge(hm_lo_ready, 10 * b + NJ * (g + 1))
                    pe.wait_ge(z_done, CREDIT + 4 * b + p)
                    if isinstance(b, int) and b == 0 and p == 0:
                        pe.wait_ge(prep, 6)
                toks = slice(P * (2 * (p % 2) + t), P * (2 * (p % 2) + t + 1))
                ps, hi, lo = ps_ffn[:, D * t:D * (t + 1)], hm_hi[g], hm_lo[g]
                split_mm(ps, [(hi[:, j, toks], lo[:, j, toks], w2_hi[:, j, :], w2_lo[:, j, :])
                              for j in range(LAST)], ended=False)
                mm(ps, hi[:, LAST, toks], w2_hi[:, LAST, :], start=False, stop=False)
                last = mm(ps, lo[:, LAST, toks], w2_last[:, :], start=False, stop=True)
                if t == 1:
                    last.then_inc(ffn_ready, 1)

            def attention(b, q, p):
                if p == 0:
                    pe.wait_ge(chain_read, CREDIT + NSTAGE * b + 12)
                if p % 2 == 0:
                    pe.wait_ge(xnT_lo_ready, 2 * b + p // 2 + 1)
                pe.wait_ge(u_done, CREDIT + 4 * b + p)
                for t in range(2):
                    toks = slice(P * (2 * p + t), P * (2 * p + t + 1))
                    last = split_mm(ps_attn[:, D * t:D * (t + 1)],
                                    [(xnT_hi[:, c, toks], xnT_lo[:, c, toks], attn_hi[:, c, :], attn_lo[:, c, :])
                                     for c in range(DC)])
                last.then_inc(attn_ready, 1)

            def square(ps, lhs, rhs):
                for m in range(DC):
                    for c in range(DC):
                        last = mm(ps[:, D * m:D * (m + 1)], lhs(c, m), rhs(c), start=(c == 0), stop=(c == DC - 1))
                return last

            def chunk(m):
                return slice(P * m, P * (m + 1))

            def chain(b, q, s):
                if s == 0:
                    pe.wait_ge(tok_sum_ready, b + 1)
                pe.wait_ge(chain_read, CREDIT + NSTAGE * b + s)
                ps = ps_chain
                if s == 0:
                    for c in range(DC):
                        last = mm(ps[:, chunk(c)], tok_sum[:, c:c + 1].to_broadcast([P, P]), ident, start=True,
                                  stop=True)
                elif s == 1:
                    for c in range(DC):
                        last = mm(ps[0:RS, 0:D], tok_sum[:, c:c + 1].to_broadcast([P, RS]), wqkvT_sb[:, c, 2 * D:3 * D],
                                  start=(c == 0), stop=(c == DC - 1))
                    last.then_inc(chain_pe, 1)
                    for c in range(DC):
                        last = mm(ps_gram[:, D * c:D * (c + 1)], sum_rows[:, 0, chunk(c)], sum_rows[:, 1, :], start=False,
                                  stop=(c == DC - 1), skip_group_check=True)
                    last.then_inc(gram_done, 1)
                    return
                elif s == 2:
                    pe.wait_ge(gram_read, b + 1)
                    for m in range(DC):
                        for c in range(DC):
                            last = nc.tensor.transpose(ps[:, D * m + P * c:D * m + P * (c + 1)], gram[:, c, chunk(m)],
                                                       ident)
                elif s == 3:
                    for m in range(DC):
                        for c in range(DC):
                            mm(ps[:, D * m:D * (m + 1)], gram[:, c, chunk(m)], wqkvT_sb[:, c, 2 * D:3 * D],
                               start=(c == 0), stop=False)
                        last = mm(ps[:, D * m:D * (m + 1)], sum_rows[:, 0, chunk(m)], v_parts[:, :], start=False,
                                  stop=True)
                elif s == 4:
                    for m in range(DC):
                        for c in range(DC):
                            mm(ps[:, chunk(m)], wqkvT_sb[:, c, D + P * m:D + P * (m + 1)], gram_v[:, c, chunk(m)],
                               start=(c == 0), stop=False)
                        last = mm(ps[:, chunk(m)], bk_parts[:, chunk(m)], v_parts[:, chunk(m)], start=False, stop=True)
                elif s == 5:
                    for c in range(DC):
                        last = mm(ps[:, D * c:D * (c + 1)], kv[:, c, :], wq_sb[:, c, :], start=True, stop=True)
                elif s == 6:
                    for m in range(DC):
                        for c in range(DC):
                            last = mm(ps[:, D * m + P * c:D * m + P * (c + 1)], wq_sb[:, c, chunk(m)], kv[:, c, :],
                                      start=True, stop=True)
                elif s == 7:
                    last = square(ps, lambda c, m: map_[:, c, chunk(m)], lambda c: gram[:, c, :])
                elif s == 8:
                    for c in range(DC):
                        last = mm(ps[:, c:c + 1], kv[:, c, :], bq_col[:, c:c + 1], start=True, stop=True)
                elif s == 9:
                    last = mm(ps[:, 0:DC], head_mean, stat[:, 2:6:2], start=True, stop=True)
                elif s == 10:
                    last = mm(ps[:, 0:DC], head_mean, second[:, :], start=True, stop=True)
                elif s == 11:
                    pe.wait_ge(scaled_ready, b + 1)
                    last = square(ps, lambda c, m: mapT[:, c, chunk(m)], lambda c: outw_scaled[:, c, :])
                else:
                    for c in range(DC):
                        last = mm(ps[:, 0:D], gn_shift[:, c:c + 1].to_broadcast([P, P]), outwT_sb[:, c, :],
                                  start=(c == 0), stop=(c == DC - 1))
                last.then_inc(chain_pe, 1)

            def first(nb, half, q):
                pe.wait_ge(consts_in, 32)
                for c in range(DC):
                    transposes(nb, q, 0, c)
                gram_tiles(nb, q, 0, 0)
                for c in range(DC):
                    transposes(nb, q, 1, c)
                gram_tiles(nb, q, 0, 1)
                bias_products()
                for h in range(2):
                    gram_tiles(nb, q, 1, h)
                pe.wait_ge(prep, 2)
                pe.wait_ge(w1_split, 1)
                pe.wait_ge(weights_in, 16 * WEIGHT_DMAS)

            def step(b, q, nxt, prev):
                chain(b, q, 0)
                if prev is not None:
                    ffn(prev, 2, 0)
                    ffn(prev, 2, 1)
                hidden(b, 0, 0)
                chain(b, q, 1)
                if prev is not None:
                    ffn(prev, 3, 0)
                scores(b, 0)
                chain(b, q, 2)
                hidden(b, 0, 1)
                route(b, 0)
                if prev is not None:
                    attention(prev, 1 - q, 2)
                chain(b, q, 3)
                if prev is not None:
                    ffn(prev, 3, 1)
                chain(b, q, 4)
                hidden(b, 0, 2)
                hidden(b, 0, 3)
                if prev is not None:
                    attention(prev, 1 - q, 3)
                if nxt:
                    transposes(nxt[0], 1 - q, 0, 0)
                chain(b, q, 5)
                hidden(b, 0, 4)
                chain(b, q, 6)
                hidden(b, 1, 0)
                chain(b, q, 7)
                scores(b, 1)
                if nxt:
                    gram_tiles(nxt[0], 1 - q, 0, 0)
                chain(b, q, 8)
                hidden(b, 1, 1)
                if nxt:
                    gram_tiles(nxt[0], 1 - q, 0, 1)
                chain(b, q, 9)
                route(b, 1)
                ffn(b, 0, 0)
                chain(b, q, 10)
                if nxt:
                    transposes(nxt[0], 1 - q, 0, 1)
                ffn(b, 0, 1)
                hidden(b, 1, 2)
                hidden(b, 1, 3)
                if nxt:
                    transposes(nxt[0], 1 - q, 1, 0)
                chain(b, q, 11)
                if nxt:
                    transposes(nxt[0], 1 - q, 1, 1)
                hidden(b, 1, 4)
                ffn(b, 1, 0)
                chain(b, q, 12)
                attention(b, q, 0)
                ffn(b, 1, 1)
                if nxt:
                    gram_tiles(nxt[0], 1 - q, 1, 0)
                attention(b, q, 1)
                if nxt:
                    gram_tiles(nxt[0], 1 - q, 1, 1)

            def tail(b, q):
                ffn(b, 2, 0)
                ffn(b, 2, 1)
                attention(b, q, 2)
                ffn(b, 3, 0)
                ffn(b, 3, 1)
                attention(b, q, 3)

            batches(pe, first, step, tail)


def h_flat(t):
    return t[:, :, :].rearrange("p j n -> p (j n)")


def kernel(**inputs):
    import numpy as np
    import concourse.bacc as bacc
    from concourse.bass_utils import run_bass_kernel_spmd

    a = {n.replace("L0_", ""): np.asarray(v) for n, v in inputs.items()}
    f = np.float32
    D = a["attn_x"].shape[2]
    E, DM = a["ffn_b1"].shape
    NJ = (E + 1) * DM // P
    DH = 8

    def as_cols(v):
        return v.reshape(-1, P).T

    b1 = np.zeros((NJ * P,), f)
    b1[:E * DM] = a["ffn_b1"].reshape(-1)
    bo1 = np.zeros((P,), f)
    bo1[DM:] = a["ffn_bo1"]
    cols = np.concatenate([as_cols(a["attn_Wqkv_b"][:D]), as_cols(a["attn_gn_w"]), as_cols(a["attn_gn_b"])]
                          + [as_cols(a["ffn_mix_kernel"][j]) for j in range(3)] + [as_cols(b1), as_cols(bo1)], 1)
    rows = np.tile(a["attn_Wqkv_b"][D:], (65, 1))

    same_head = (np.arange(P)[:, None] // DH == np.arange(P)[None, :] // DH).astype(f)
    feature_path = np.arange(NJ * P) // DM
    path_of = (feature_path[:, None] == np.arange(E)[None, :]).astype(f)
    feature_rank = (E - feature_path).astype(f)
    feature_rank[E * DM:] = 0
    for at in (E * DM, E * DM + 32):
        feature_rank[at:at + E] = np.arange(E, 0, -1)
    part_rows = np.zeros((P, 1), f)
    part_rows[0:65:32] = 1
    consts = np.concatenate([np.eye(P, dtype=f), same_head, same_head / DH, np.ones((P, 1), f),
                             np.full((P, 1), -0.5, f), np.tile(np.arange(E, 0, -1, dtype=f), (P, 1)),
                             as_cols(feature_rank), part_rows,
                             path_of.reshape(NJ, P, E).transpose(1, 0, 2).reshape(P, NJ * E)], 1)

    arrays = {
        "x": a["attn_x"],
        "wqkv_t": a["attn_Wqkv_w"].T,
        "wq": a["attn_Wqkv_w"][:D],
        "out_wt": a["attn_out_w"].T,
        "w1": np.concatenate([a["ffn_W1"].transpose(1, 0, 2).reshape(D, E * DM), a["ffn_Wo1"]], 1),
        "w2": a["ffn_W2"].reshape(E * DM, D),
        "wo2": a["ffn_Wo2"],
        "b2": a["ffn_b2"],
        "cols": cols,
        "rows": rows,
        "gamma": np.tile(a["ffn_gamma"], (P, 1)),
        "beta": np.tile(a["ffn_beta"], (P, 1)),
        "out_b": np.tile(a["attn_out_b"], (P, 1)),
        "bo2": np.tile(a["ffn_bo2"], (P, 1)),
        "consts": consts,
    }
    nc = bacc.Bacc("TRN2", target_bir_lowering=False, num_devices=1)
    given, args = {}, []
    for name, v in arrays.items():
        given[name] = np.ascontiguousarray(v)
        args.append(nc.dram_tensor(name, v.shape, mybir.dt.from_np(v.dtype), kind="ExternalInput").ap())
    out = nc.dram_tensor("out", a["attn_x"].shape, F32, kind="ExternalOutput").ap()
    block_kernel(nc, *args, out)
    r = run_bass_kernel_spmd(nc, [given], core_ids=[0])
    return r.results[0]["out"]
```
